# Optimizing a Trainium2 kernel written in Bass

```python
import numpy as np
import jax
import jax.numpy as jnp

def _softmax(x, axis=-1):
    return jax.nn.softmax(x, axis=axis)

def _gelu(x):
    return jax.nn.gelu(x, approximate=True)

def _silu(x):
    return jax.nn.silu(x)

def _sigmoid(x):
    return jax.nn.sigmoid(x)

def _layernorm(x, axis=-1, eps=1e-05):
    m = jnp.mean(x, axis=axis, keepdims=True)
    v = jnp.var(x, axis=axis, keepdims=True)
    return (x - m) / jnp.sqrt(v + eps)

def _scatter_add(tgt, idx, src, axis=0):
    return tgt.at[idx].add(src)

def _segment_sum(src, seg, n):
    return jax.ops.segment_sum(src, seg, n)
kernel_name = 'mk_lm_tower_d1_tok_ids1024_r4_8da2a8'

def setup_inputs(seed: int=0):
    np.random.seed(seed)
    _w = jnp.asarray

    def _rec_inputs():
        import jax
        import jax.numpy as jnp
        _rk = jax.random.key(seed)
        x = jax.random.randint(jax.random.fold_in(_rk, 1), (16, 256), 0, 12564, jnp.int32)
        return x
    x = _rec_inputs()

    def _L0_tok_setup():
        import jax, jax.numpy as jnp
        import numpy as np
        NUM_EMB = 50257
        EMB_DIM = 256
        RANK = 8
        LORA_ALPHA = 8
        SCALING = LORA_ALPHA / RANK ** 0.5
        key = jax.random.key(seed)
        k1, k2, k3, k4 = jax.random.split(key, 4)
        x = jax.random.randint(k1, (8, 1024), 0, NUM_EMB, dtype=jnp.int64)
        weight = jax.random.normal(k2, (NUM_EMB, EMB_DIM), dtype=jnp.float32)
        bound = float(np.sqrt(3.0) * np.sqrt(2.0 / 6.0) / np.sqrt(RANK))
        lora_A = jax.random.uniform(k3, (NUM_EMB, RANK), dtype=jnp.float32, minval=-bound, maxval=bound)
        lora_B = jax.random.normal(k4, (RANK, EMB_DIM), dtype=jnp.float32) * 0.02
        return {'x': x, 'weight': weight, 'lora_A': lora_A, 'lora_B': lora_B}
    _L0_tok_all = _L0_tok_setup()
    _L0_tok_in = {k: v for k, v in _L0_tok_all.items() if k in ('weight', 'lora_A', 'lora_B')}
    del _L0_tok_all

    def _L0_attn_setup():
        import math
        import jax, jax.numpy as jnp
        import numpy as np
        B, T, C, H = (8, 256, 256, 16)
        HD = C // H
        key = jax.random.key(seed)
        ks = jax.random.split(key, 7)
        return {'x': jax.random.normal(ks[0], (B, T, C), dtype=jnp.float32), 'Wattn': jax.random.normal(ks[1], (C, 3 * C), dtype=jnp.float32) * 0.02, 'battn': jax.random.normal(ks[2], (3 * C,), dtype=jnp.float32) * 0.02, 'Wproj': jax.random.normal(ks[3], (C, C), dtype=jnp.float32) * 0.02, 'bproj': jax.random.normal(ks[4], (C,), dtype=jnp.float32) * 0.02, 'embk': jax.random.normal(ks[5], (T, HD), dtype=jnp.float32) * 0.02, 'embv': jax.random.normal(ks[6], (T, HD), dtype=jnp.float32) * 0.02}
    _L0_attn_all = _L0_attn_setup()
    _L0_attn_in = {k: v for k, v in _L0_attn_all.items() if k in ('Wattn', 'battn', 'Wproj', 'bproj', 'embk', 'embv')}
    del _L0_attn_all

    def _L0_ffn_setup():
        import jax, jax.numpy as jnp
        import numpy as np
        DIM = 256
        DEPTH = 7
        PAR = 8
        N_NODES = 2 ** (DEPTH + 1) - 1
        WIDTH = PAR * N_NODES
        key = jax.random.key(seed)
        k1, k2, k3, k4 = jax.random.split(key, 4)
        init_k = float(np.sqrt(1.0 / DIM))
        init_k2 = float(np.sqrt(1.0 / ((DEPTH + 1) * PAR)))
        oldx = jax.random.normal(k1, (4, 512, DIM), dtype=jnp.float32)
        W_in = jax.random.uniform(k2, (WIDTH, DIM), jnp.float32, -init_k, init_k)
        b_in = jax.random.uniform(k3, (WIDTH,), jnp.float32, -init_k, init_k)
        W_out = jax.random.uniform(k4, (DIM, WIDTH), jnp.float32, -init_k2, init_k2)
        return {'oldx': oldx, 'W_in': W_in, 'b_in': b_in, 'W_out': W_out}
    _L0_ffn_all = _L0_ffn_setup()
    _L0_ffn_in = {k: v for k, v in _L0_ffn_all.items() if k in ('W_in', 'b_in', 'W_out')}
    del _L0_ffn_all
    return {'x': x, 'L0_tok_weight': _L0_tok_in['weight'], 'L0_tok_lora_A': _L0_tok_in['lora_A'], 'L0_tok_lora_B': _L0_tok_in['lora_B'], 'L0_attn_Wattn': _L0_attn_in['Wattn'], 'L0_attn_battn': _L0_attn_in['battn'], 'L0_attn_Wproj': _L0_attn_in['Wproj'], 'L0_attn_bproj': _L0_attn_in['bproj'], 'L0_attn_embk': _L0_attn_in['embk'], 'L0_attn_embv': _L0_attn_in['embv'], 'L0_ffn_W_in': _L0_ffn_in['W_in'], 'L0_ffn_b_in': _L0_ffn_in['b_in'], 'L0_ffn_W_out': _L0_ffn_in['W_out']}

def reference(x, L0_tok_weight, L0_tok_lora_A, L0_tok_lora_B, L0_attn_Wattn, L0_attn_battn, L0_attn_Wproj, L0_attn_bproj, L0_attn_embk, L0_attn_embv, L0_ffn_W_in, L0_ffn_b_in, L0_ffn_W_out):
    import jax
    import jax.numpy as jnp

    def _L0_tok_ref(x, weight, lora_A, lora_B):
        import jax, jax.numpy as jnp
        import numpy as np
        NUM_EMB = 50257
        EMB_DIM = 256
        RANK = 8
        LORA_ALPHA = 8
        SCALING = LORA_ALPHA / RANK ** 0.5
        base_out = weight[x]
        lora_out = jnp.einsum('bsr,rd->bsd', lora_A[x], lora_B)
        return base_out + lora_out * SCALING

    def _L0_attn_ref(x, Wattn, battn, Wproj, bproj, embk, embv):
        import math
        import jax, jax.numpy as jnp
        import numpy as np
        B, T, C, H = (8, 256, 256, 16)
        HD = C // H
        b, t, c = x.shape
        qkv = x @ Wattn + battn
        q, k, v = jnp.split(qkv, 3, axis=-1)
        q = q.reshape(b, t, H, HD).transpose(0, 2, 1, 3)
        k = k.reshape(b, t, H, HD).transpose(0, 2, 1, 3)
        v = v.reshape(b, t, H, HD).transpose(0, 2, 1, 3)
        idx = jnp.arange(t)
        rel = jnp.tril(idx[:, None] - idx[None, :])
        rk = embk[rel]
        rv = embv[rel]
        scale = 1.0 / math.sqrt(HD)
        att1 = jnp.einsum('bhtd,bhsd->bhts', q, k) * scale
        att2 = jnp.einsum('bhtd,tsd->bhts', q, rk)
        att = att1 + att2
        causal = idx[None, :] <= idx[:, None]
        att = jnp.where(causal[None, None], att, -jnp.inf)
        att = jax.nn.softmax(att, axis=-1)
        y1 = jnp.einsum('bhts,bhsd->bhtd', att, v)
        y2 = jnp.einsum('bhts,tsd->bhtd', att, rv)
        y = (y1 + y2).transpose(0, 2, 1, 3).reshape(b, t, c)
        return y @ Wproj + bproj

    def _L0_ffn_ref(oldx, W_in, b_in, W_out):
        import jax, jax.numpy as jnp
        import numpy as np
        DIM = 256
        DEPTH = 7
        PAR = 8
        N_NODES = 2 ** (DEPTH + 1) - 1
        WIDTH = PAR * N_NODES
        x = oldx.reshape(-1, DIM)
        B = x.shape[0]
        logits = x @ W_in.T + b_in
        decisions = (logits > 0).astype(jnp.int32).reshape(B, PAR, N_NODES)
        acts = jax.nn.silu(logits).reshape(B, PAR, N_NODES)
        current = jnp.zeros((B, PAR), dtype=jnp.int32)
        dmap = jax.nn.one_hot(current, N_NODES, dtype=acts.dtype)
        for d in range(DEPTH):
            cur_platform = 2 ** d - 1
            next_platform = 2 ** (d + 1) - 1
            moves = jnp.take_along_axis(decisions, current[..., None], axis=2)[..., 0]
            current = (current - cur_platform) * 2 + moves + next_platform
            dmap = dmap + jax.nn.one_hot(current, N_NODES, dtype=acts.dtype)
        masked = acts * jax.lax.stop_gradient(dmap)
        out = masked.reshape(B, WIDTH) @ W_out.T
        return out.reshape(oldx.shape)
    h = _L0_tok_ref(x, L0_tok_weight, L0_tok_lora_A, L0_tok_lora_B)
    h = h + _L0_attn_ref(_layernorm(h, axis=-1), L0_attn_Wattn, L0_attn_battn, L0_attn_Wproj, L0_attn_bproj, L0_attn_embk, L0_attn_embv)
    h = h + _L0_ffn_ref(_layernorm(h, axis=-1), L0_ffn_W_in, L0_ffn_b_in, L0_ffn_W_out)
    return h

_drawn_inputs = setup_inputs


def setup_inputs(seed=0):
    import zlib

    import numpy as np

    out = dict(_drawn_inputs(seed))
    spreads = {}
    factors = {'L0_attn_embk': 36.657, 'L0_attn_embv': 8.0, 'L0_attn_battn': 2.667}
    for name, (base, spread) in spreads.items():
        noise = np.random.default_rng([zlib.crc32(name.encode()), seed]).standard_normal(out[name].shape)
        drawn = base * np.exp(spread * noise) if base else spread * noise
        out[name] = jnp.asarray(drawn.astype(out[name].dtype))
    for name, factor in factors.items():
        out[name] = (out[name] * factor).astype(out[name].dtype)
    return out
```

```python
import math
import numpy as np
import concourse.bass as bass
from concourse import mybir
from contextlib import ExitStack

F32 = mybir.dt.float32
BF16 = mybir.dt.bfloat16
U32 = mybir.dt.uint32
ALU = mybir.AluOpType
ACT = mybir.ActivationFunctionType
AX = mybir.AxisListType

P = 128
BATCH, T, C, H = 16, 256, 256, 16
HD = C // H
TOK = BATCH * T
G = 8
GT = TOK // G
TILES = GT // P
GB = GT // T
BH = GB * H
CM = C // P
RANK = 8
LORA_SCALE = 8 / math.sqrt(RANK)
QK_SCALE = 1 / math.sqrt(HD)
EPS = 1e-5
PAR, DEPTH = 8, 7
WT = 2 * PAR
Q_PARTS = (0, 0, 1, 1, 0, 2)
K_PARTS = (0, 1, 0, 1, 2, 0)
KS = len(Q_PARTS) * HD
MASK = -1e30
SPAN = T + P
BLOCK = 8
JC = 16
QT = T // 4


def need(eng, sem, count):
    if not (isinstance(count, int) and count <= 0):
        eng.wait_ge(sem, count)


def apart(eng, waits_done):
    eng.sem_inc(waits_done, 1)


def groups(eng, prologue, body, epilogue):
    prologue()
    body(0, 0, 0)
    with eng.Fori(0, 3) as i:
        body(i * 2 + 1, i, 1)
        body(i * 2 + 2, i + 1, 0)
    epilogue(G - 1, G // 2 - 1, 1)


def tower_kernel(nc, idx, tok_w, lora_a, lora_b, wattn, battn, vbias, wproj, bproj, embk_rev, embv_pad,
                 w_in, b_in, w_out, ident_in, tree_in, thr_in, out):
    ctx = ExitStack()
    with ctx:
        def sb(name, shape, dt=F32):
            return ctx.enter_context(nc.sbuf_tensor(name, shape, dt))

        def sem(name):
            return ctx.enter_context(nc.semaphore(name))

        def two(name):
            return [sem(f"{name}{n}") for n in range(2)]

        h_d = nc.dram_tensor("h_d", (TOK, C), F32, kind="Internal").ap()
        h2_d = nc.dram_tensor("h2_d", (TOK, C), F32, kind="Internal").ap()
        v_d = nc.dram_tensor("v_d", (TOK, C), F32, kind="Internal").ap()
        qk_d = nc.dram_tensor("qk_d", (2, 3, C, TOK), BF16, kind="Internal").ap()
        y1_d = nc.dram_tensor("y1_d", (C, TOK), F32, kind="Internal").ap()
        y2_d = nc.dram_tensor("y2_d", (C, TOK), F32, kind="Internal").ap()

        ps = ctx.enter_context(nc.psum_tensor("ps", [P, 8, 512], F32))

        def rows(dram, g):
            return dram[bass.ds(g * GT, GT), :].rearrange("(i p) c -> p i c", p=P)

        ident = sb("ident", [P, P])
        small = sb("small", [P, 32])
        consts = sem("consts")
        kb_ready = sem("kb_ready")
        psum_clear = sem("psum_clear")
        CONSTS = 16 * 5

        sp_waited, pool_waited, dve_waited = sem("sp_waited"), sem("pool_waited"), sem("dve_waited")

        idx_sb = sb("idx_sb", [P, TOK // P], mybir.dt.int32)
        idx_g = [sb(f"idx_g{n}", [P, TILES], mybir.dt.int32) for n in range(2)]
        idx_loaded, idx_ready = sem("idx_loaded"), sem("idx_ready")

        stage1 = ExitStack()

        def sb1(name, shape, dt=F32):
            return stage1.enter_context(nc.sbuf_tensor(name, shape, dt))

        w_loaded = sem("w_loaded")
        gathered = two("gathered")
        a_transposed, at_copied, lora_ready, h_made = (sem(n) for n in ("a_transposed", "at_copied", "lora_ready", "h_made"))
        var_ready, std_ready, xn_ready, x_transposed, xt_ready = (sem(n) for n in ("var_ready", "std_ready", "xn_ready", "x_transposed", "xt_ready"))
        qk_full, qk_copied, qk_part1, qk_rest, qk_part2, qk_part3 = (sem(n) for n in ("qk_full", "qk_copied", "qk_part1", "qk_rest", "qk_part2", "qk_part3"))
        v_full, v_copied = sem("v_full"), sem("v_copied")
        h_stored, v_stored, parts_stored = two("h_stored"), two("v_stored"), two("parts_stored")
        dve_chain = sem("dve_chain")

        wa = sb1("wa", [P, CM, 3 * C])
        vb = sb1("vb", [P, C])
        lb = sb1("lb", [RANK, C])
        staged = [sb1(f"staged{n}", [P, TILES, C]) for n in range(2)]
        staged_a = [sb1(f"staged_a{n}", [P, TILES, RANK]) for n in range(2)]
        at = sb1("at", [RANK, GT])
        h_new = [sb1(f"h_new{n}", [P, TILES, C]) for n in range(2)]
        stats = sb1("stats", [P, TILES, 6])
        mv = sb1("mv", [P, TILES, 2])
        ln = sb1("ln", [P, 4, TILES])
        xn = sb1("xn", [P, TILES, C])
        xt = [sb1(f"xt{n}", [P, CM, GT]) for n in range(2)]
        x32 = [sb1(f"x32_{n}", [P, GT]) for n in range(2)]
        rest = [sb1(f"rest{n}", [P, GT]) for n in range(2)]
        parts = [sb1(f"parts{n}", [P, 3, GT], BF16) for n in range(2)]
        v_out = [sb1(f"v_out{n}", [P, TILES, C]) for n in range(2)]
        STAGE1_STORES = None
        stage1_stored = [(h_stored, 16 * G // 2), (v_stored, 16 * G // 2), (parts_stored, 16 * 2 * G)]
        LN_LINKS = 7

        def layer_norm(dve, call, src, st, mvt, lnt, dst, variance, std, done, chain):
            n = [call * LN_LINKS]

            def link(ins):
                n[0] = n[0] + 1
                ins.then_inc(chain, 1)
                dve.wait_ge(chain, n[0])

            for i in range(TILES):
                ins = nc.vector.bn_stats(st[:, i, :], src[:, i, :])
            link(ins)
            apart(dve, dve_waited)
            for i in range(TILES):
                ins = nc.vector.bn_aggr(mvt[:, i, :], st[:, i, :])
            link(ins)
            nc.vector.tensor_scalar(lnt[:, 0, :], mvt[:, :, 1], EPS, None, ALU.add).then_inc(variance, 1)
            dve.wait_ge(std, call + 1)
            link(nc.vector.reciprocal(lnt[:, 2, :], lnt[:, 1, :]))
            link(nc.vector.tensor_tensor(lnt[:, 3, :], lnt[:, 2, :], lnt[:, 2, :], ALU.mult))
            link(nc.vector.tensor_tensor(lnt[:, 3, :], lnt[:, 3, :], lnt[:, 0, :], ALU.mult))
            link(nc.vector.tensor_scalar(lnt[:, 3, :], lnt[:, 3, :], -0.5, 1.5, ALU.mult, ALU.add))
            link(nc.vector.tensor_tensor(lnt[:, 2, :], lnt[:, 2, :], lnt[:, 3, :], ALU.mult))
            for i in range(TILES):
                ins = nc.vector.tensor_scalar(dst[:, i, :], src[:, i, :], mvt[:, i, 0:1], lnt[:, 2, i:i + 1],
                                              ALU.subtract, ALU.mult)
            link_last = ins
            link_last.then_inc(done, 1)

        stage1.close()
        stage2 = ExitStack()

        def sb2(name, shape, dt=F32):
            return stage2.enter_context(nc.sbuf_tensor(name, shape, dt))

        stage1_done = sem("stage1_done")
        att = [sb2(f"att{n}", [P, BH, SPAN]) for n in range(2)]
        q_stack = [sb2(f"q_stack{n}", [KS + 1, BH, T], BF16) for n in range(2)]
        k_stack = sb2("k_stack", [KS, BH, T], BF16)
        r_stack = sb2("r_stack", [KS + 1, SPAN], BF16)
        ekp = sb2("ekp", [HD, 3, T], BF16)
        rv = sb2("rv", [P, T, HD])
        wp = sb2("wp", [P, CM, C])
        bp = sb2("bp", [P, C])
        v_in = [sb2(f"v_in{n}", [P, TILES, C]) for n in range(2)]
        neg_max = sb2("neg_max", [P, BH, 3])
        sums = [sb2(f"sums{n}", [P, H, GB, 2]) for n in range(2)]
        probs = [sb2(f"probs{n}", [P, SPAN]) for n in range(2)]
        y1s = sb2("y1s", [P, H // 4, GT])
        y2s = sb2("y2s", [P, BH, QT])
        ek = y1s[0:HD, 0, :].rearrange("d (n t) -> d n t", n=2)
        y1c = sb2("y1c", [P, CM, GT])
        y2c = sb2("y2c", [P, CM, GT])
        yn = sb2("yn", [P, TILES, C])
        yt = y2c
        hin = y1c[:, :, :].rearrange("p m t -> p (m t)").rearrange("p (i c) -> p i c", i=TILES)

        w2_loaded, ek_loaded, ek_split, ek_stacked = sem("w2_loaded"), sem("ek_loaded"), sem("ek_split"), sem("ek_stacked")
        ones_ready = sem("ones_ready")
        q_loaded, v_loaded = two("q_loaded"), two("v_loaded")
        k_loaded, h_loaded = sem("k_loaded"), sem("h_loaded")
        att2_full, att2_copied, att1_full, scores_ready = (sem(n) for n in ("att2_full", "att2_copied", "att1_full", "scores_ready"))
        st_full, maxes, max_ready, exp_done, pt_full = (sem(n) for n in ("st_full", "maxes", "max_ready", "exp_done", "pt_full"))
        pt_copied = two("pt_copied")
        y1_full, y1_copied, y1_stored, y2_full, y2_copied, y2_stored = (sem(n) for n in ("y1_full", "y1_copied", "y1_stored", "y2_full", "y2_copied", "y2_stored"))
        yc_loaded, y_summed, inv_ready = sem("yc_loaded"), sem("y_summed"), sem("inv_ready")
        y_back, yn_ready, yt_full, yt_copied, proj_full, proj_ready, h2_ready, h2_stored = (
            sem(n) for n in ("y_back", "yn_ready", "yt_full", "yt_copied", "proj_full", "proj_ready", "h2_ready", "h2_stored"))
        A_USES = SPAN // JC

        stage2.close()
        stage3 = ExitStack()

        def sb3(name, shape, dt=F32):
            return stage3.enter_context(nc.sbuf_tensor(name, shape, dt))

        wi = sb3("wi", [P, CM, WT * P])
        wo = sb3("wo", [P, WT, C])
        treef = sb3("treef", [P, 2 * P])
        tree = sb3("tree", [P, 2 * P], BF16)
        h3 = [sb3(f"h3_{n}", [P, TILES, C]) for n in range(2)]
        stats3 = sb3("stats3", [P, TILES, 6])
        mv3 = sb3("mv3", [P, TILES, 2])
        ln3 = sb3("ln3", [P, 4, TILES])
        xn3 = sb3("xn3", [P, TILES, C])
        xt3 = [sb3(f"xt3_{n}", [P, CM, GT]) for n in range(2)]
        dec = [sb3(f"dec{n}", [P, GT], BF16) for n in range(2)]
        acts = [[sb3(f"acts{n}{m}", [P, GT]) for m in range(2)] for n in range(2)]
        masked = [[sb3(f"masked{n}{m}", [P, GT]) for m in range(2)] for n in range(2)]
        o3 = [sb3(f"o3_{n}", [P, TILES, C]) for n in range(2)]
        stage3.close()
        w3_loaded, tree_ready = sem("w3_loaded"), sem("tree_ready")
        h3_loaded, out_stored = two("h3_loaded"), two("out_stored")
        var3, std3, xn3_ready, x3_transposed, xt3_ready = (sem(n) for n in ("var3", "std3", "xn3_ready", "x3_transposed", "xt3_ready"))
        logit_full, dec_ready, acts_ready, reach_full, masked_ready, ffn_full, out_ready = (
            sem(n) for n in ("logit_full", "dec_ready", "acts_ready", "reach_full", "masked_ready", "ffn_full", "out_ready"))
        stage2_done = sem("stage2_done")
        chain3 = sem("chain3")

        block = ctx.enter_context(nc.Block())

        @block.sync
        def _(sp):
            sp.dma_start(idx_sb[:], idx).then_inc(idx_loaded, 16)
            sp.dma_start(ident[:], ident_in).then_inc(consts, 16)
            sp.dma_start(small[:, 0:6], battn).then_inc(consts, 16)
            sp.dma_start(small[:, 8:8 + WT], b_in).then_inc(consts, 16)
            sp.dma_start(small[:, 24:26], thr_in).then_inc(consts, 16)
            sp.dma_start(lb[:], lora_b).then_inc(consts, 16)
            sp.dma_start(wa[:], wattn.rearrange("(m p) n -> p m n", p=P)).then_inc(w_loaded, 16)
            sp.dma_start(vb[:], vbias.to_broadcast([P, C])).then_inc(w_loaded, 16)

            def store_h(g, half, par):
                sp.wait_ge(h_made, g + 1)
                apart(sp, sp_waited)
                sp.dma_start(rows(h_d, g), h_new[par][:]).then_inc(h_stored[par], 16)

            def store_qkv(g, half, par):
                for u in range(4):
                    sp.wait_ge(qk_part3, 4 * g + u + 1)
                    apart(sp, sp_waited)
                    dst = qk_d[u // 2, :, (u % 2) * P:(u % 2 + 1) * P, bass.ds(g * GT, GT)]
                    sp.dma_start(dst.rearrange("n p t -> p n t"), parts[u % 2][:]).then_inc(parts_stored[u % 2], 16)
                sp.wait_ge(v_copied, 2 * (g + 1))
                apart(sp, sp_waited)
                sp.dma_start(rows(v_d, g), v_out[par][:]).then_inc(v_stored[par], 16)

            def body1(g, half, par):
                store_h(g + 1, half, 1 - par)
                store_qkv(g, half, par)

            groups(sp, lambda: store_h(0, 0, 0), body1, store_qkv)
            for pair, count in stage1_stored:
                for s in pair:
                    sp.wait_ge(s, count)
            sp.sem_inc(stage1_done, 1)

            for s, n in ((qk_copied, 4 * G), (x_transposed, G), (qk_full, 4 * G), (v_full, 2 * G), (v_copied, 2 * G), (qk_part3, 4 * G)):
                sp.wait_ge(s, n)
            sp.dma_start(ek[:, 0, :], embk_rev).then_inc(ek_loaded, 16)
            sp.dma_start(rv[:], bass.AP(embv_pad.tensor, 0, [[HD, P], [HD, T], [1, HD]])).then_inc(w2_loaded, 16)
            sp.dma_start(wp[:], wproj.rearrange("(m p) n -> p m n", p=P)).then_inc(w2_loaded, 16)
            sp.dma_start(bp[:], bproj.to_broadcast([P, C])).then_inc(w2_loaded, 16)

            def stack(which, dst, part_of, g, loaded):
                for n, part in enumerate(part_of):
                    src = qk_d[which, part, :, bass.ds(g * GT, GT)].rearrange("(h d) t -> d h t", d=HD)
                    sp.dma_start(dst[n * HD:(n + 1) * HD, :, :].rearrange("d (h b) t -> d h (b t)", h=H), src).then_inc(loaded, 16)

            def load_q(g, par):
                need(sp, y1_full, 4 * (g - 1))
                apart(sp, sp_waited)
                stack(0, q_stack[par], Q_PARTS, g, q_loaded[par])
                sp.dma_start(v_in[par][:], rows(v_d, g)).then_inc(v_loaded[par], 16)

            def load_k(g):
                need(sp, att1_full, BH * g)
                apart(sp, sp_waited)
                stack(1, k_stack, K_PARTS, g, k_loaded)

            def tail(g, half, par):
                sp.wait_ge(y1_copied, 4 * (g + 1))
                apart(sp, sp_waited)
                for q in range(4):
                    dst = y1_d.rearrange("(a q d) t -> q d a t", q=4, d=HD)[q][:, :, bass.ds(g * GT, GT)]
                    sp.dma_start(dst, y1s[32 * q:32 * q + HD, :, :]).then_inc(y1_stored, 16)
                sp.wait_ge(y2_copied, 4 * (g + 1))
                apart(sp, sp_waited)
                for q in range(4):
                    for b in range(GB):
                        dst = y2_d.rearrange("(h d) t -> d h t", d=HD)[:, :, bass.ds(g * GT + b * T + q * QT, QT)]
                        src = y2s[32 * q:32 * q + HD, :, :].rearrange("p (h b) t -> p b h t", b=GB)[:, b]
                        sp.dma_start(dst, src).then_inc(y2_stored, 16)
                sp.wait_ge(y1_stored, 64 * (g + 1))
                apart(sp, sp_waited)
                need(sp, h2_stored, 16 * g)
                apart(sp, sp_waited)
                sp.dma_start(y1c[:], y1_d[:, bass.ds(g * GT, GT)].rearrange("(m p) t -> p m t", p=P)).then_inc(yc_loaded, 16)
                sp.wait_ge(y2_stored, 128 * (g + 1))
                apart(sp, sp_waited)
                sp.dma_start(y2c[:], y2_d[:, bass.ds(g * GT, GT)].rearrange("(m p) t -> p m t", p=P)).then_inc(yc_loaded, 16)
                sp.wait_ge(y_back, 2 * (g + 1))
                apart(sp, sp_waited)
                sp.dma_start(hin, rows(h_d, g)).then_inc(h_loaded, 16)
                sp.wait_ge(h2_ready, g + 1)
                apart(sp, sp_waited)
                sp.dma_start(rows(h2_d, g), hin).then_inc(h2_stored, 16)

            def body2(g, half, par):
                load_q(g + 1, 1 - par)
                load_k(g + 1)
                tail(g, half, par)

            load_q(0, 0)
            load_k(0)
            sp.wait_ge(ek_split, 1)
            for n, part in enumerate(K_PARTS):
                sp.dma_start(r_stack[n * HD:(n + 1) * HD, 0:T], ekp[:, part, :]).then_inc(ek_stacked, 16)
            groups(sp, lambda: None, body2, tail)
            sp.wait_ge(h2_stored, 16 * G)

            sp.wait_ge(stage2_done, 3)
            sp.dma_start(wi[:], w_in.rearrange("(m p) n -> p m n", p=P)).then_inc(w3_loaded, 16)
            sp.dma_start(treef[:], tree_in).then_inc(w3_loaded, 16)
            sp.dma_start(wo[:], w_out.rearrange("(m p) n -> p m n", p=P)).then_inc(w3_loaded, 16)

            def load_h(g, par):
                need(sp, out_ready, g - 1)
                apart(sp, sp_waited)
                sp.dma_start(h3[par][:], rows(h2_d, g)).then_inc(h3_loaded[par], 16)

            def store(g, half, par):
                sp.wait_ge(out_ready, g + 1)
                apart(sp, sp_waited)
                sp.dma_start(rows(out, g), o3[par][:]).then_inc(out_stored[par], 16)

            def body3(g, half, par):
                load_h(g + 1, 1 - par)
                store(g, half, par)

            groups(sp, lambda: load_h(0, 0), body3, store)
            for s in out_stored:
                sp.wait_ge(s, 16 * G // 2)

        @block.gpsimd
        def _(pool):
            pool.wait_ge(idx_loaded, 16)

            def gather(g, half, par):
                need(pool, h_made, g - 1)
                apart(pool, pool_waited)
                nc.gpsimd.tensor_copy(idx_g[par][:], idx_sb[:, bass.ds(g * TILES, TILES)]).then_inc(idx_ready, 1)
                pool.wait_ge(idx_ready, g + 1)
                apart(pool, pool_waited)
                for i in range(TILES):
                    off = bass.IndirectOffsetOnAxis(ap=idx_g[par][:, i:i + 1].bitcast(U32), axis=0)
                    pool.indirect_dma_start(staged[par][:, i, :], None, tok_w, off).then_inc(gathered[par], 16)
                    pool.indirect_dma_start(staged_a[par][:, i, :], None, lora_a, off).then_inc(gathered[par], 16)

            def split(g, half, par):
                for u in range(4):
                    pool.wait_ge(qk_copied, 4 * g + u + 1)
                    need(pool, parts_stored[u % 2], 16 * (2 * g + u // 2))
                    apart(pool, pool_waited)
                    nc.gpsimd.tensor_copy(parts[u % 2][:, 0, :], x32[u % 2][:]).then_inc(qk_part1, 1)
                    pool.wait_ge(qk_rest, 4 * g + u + 1)
                    apart(pool, pool_waited)
                    nc.gpsimd.tensor_copy(parts[u % 2][:, 1, :], rest[u % 2][:]).then_inc(qk_part2, 1)

            def body1(g, half, par):
                gather(g + 1, half, 1 - par)
                split(g, half, par)

            groups(pool, lambda: gather(0, 0, 0), body1, split)

            pool.wait_ge(stage1_done, 1)
            for n in range(2):
                nc.gpsimd.memset(q_stack[n][KS:KS + 1, :, :], 1.0).then_inc(ones_ready, 1)
            nc.gpsimd.memset(r_stack[0:KS, T:SPAN], 0.0).then_inc(ones_ready, 1)
            nc.gpsimd.memset(r_stack[KS:KS + 1, 0:T], 0.0).then_inc(ones_ready, 1)
            nc.gpsimd.memset(r_stack[KS:KS + 1, T:SPAN], MASK).then_inc(ones_ready, 1)

            def tail(g, half, par):
                pool.wait_ge(yc_loaded, 32 * (g + 1))
                nc.gpsimd.tensor_tensor(y1c[:], y1c[:], y2c[:], ALU.add).then_inc(y_summed, 1)
                pool.wait_ge(h_loaded, 16 * (g + 1))
                pool.wait_ge(proj_ready, 2 * (g + 1))
                nc.gpsimd.tensor_tensor(hin, hin, yn[:], ALU.add).then_inc(h2_ready, 1)

            groups(pool, lambda: None, tail, tail)

        @block.scalar
        def _(act):
            def front1(g, half, par):
                act.wait_ge(a_transposed, g + 1)
                nc.scalar.activation(at[:], ps[0:RANK, 0, :], ACT.Copy).then_inc(at_copied, 1)
                act.wait_ge(var_ready, g + 1)
                nc.scalar.activation(ln[:, 1, :], ln[:, 0, :], ACT.Sqrt).then_inc(std_ready, 1)
                act.wait_ge(x_transposed, g + 1)
                nc.scalar.activation(xt[par][:], ps[:, 3:5, :], ACT.Copy).then_inc(xt_ready, 1)

            def back1(g, u0, u1):
                for u in range(u0, u1):
                    act.wait_ge(qk_full, 4 * g + u + 1)
                    need(act, qk_part3, 4 * g + u - 1)
                    need(act, qk_part1, 4 * g + u - 1)
                    bias = small[:, u:u + 1] if u < 2 else small[:, 4 + u:5 + u]
                    nc.scalar.activation(x32[u % 2][:], ps[:, 5 + u % 2, :], ACT.Identity, bias=bias,
                                         scale=1.0 if u < 2 else QK_SCALE).then_inc(qk_copied, 1)

            def body1(g, half, par):
                back1(g, 0, 2)
                front1(g + 1, half, 1 - par)
                back1(g, 2, 4)

            act.wait_ge(consts, CONSTS)
            act.wait_ge(kb_ready, 1)
            groups(act, lambda: front1(0, 0, 0), body1, lambda g, half, par: back1(g, 0, 4))

            act.wait_ge(stage1_done, 1)

            def copy_att2(g, half, par):
                need(act, y2_full, 4 * (g - 1))
                for n in range(A_USES):
                    act.wait_ge(att2_full, A_USES * g + n + 1)
                    nc.scalar.activation(att[par][:, :, n * JC:(n + 1) * JC],
                                         ps[:, n % 2, :].rearrange("p (j x) -> p x j", x=BH), ACT.Copy).then_inc(att2_copied, 1)

            def exps(g, half, par, x):
                act.wait_ge(max_ready, BH * g + x + 1)
                need(act, pt_full, BH * g + x - 1)
                sc, pr = ps[:, 2 + x % 2, :], probs[x % 2]
                h, b = x // GB, x % GB
                nc.scalar.activation(pr[:, 0:P], sc[:, 0:P], ACT.Exp, bias=neg_max[:, x, 0:1],
                                     accum_out=sums[par][:, h, b, 0:1])
                nc.scalar.activation(pr[:, P:SPAN], sc[:, P:SPAN], ACT.Exp, bias=neg_max[:, x, 1:2],
                                     accum_out=sums[par][:, h, b, 1:2]).then_inc(exp_done, 1)

            def copy_pt(g, half, par, x):
                act.wait_ge(pt_full, BH * g + x + 1)
                nc.scalar.activation(att[par][:, x, :], ps[:, 4 + x % 2, 0:SPAN], ACT.Copy).then_inc(pt_copied[1], 1)

            def copy_y1(g, nb):
                act.wait_ge(y1_full, 4 * g + nb + 1)
                need(act, y1_stored, 64 * g)
                nc.scalar.activation(y1s[:, nb, :], ps[:, 6, :], ACT.Copy).then_inc(y1_copied, 1)

            def tail_yt(g, m):
                act.wait_ge(yt_full, 2 * g + m + 1)
                nc.scalar.activation(yt[:, m, :], ps[:, 7, :], ACT.Copy).then_inc(yt_copied, 1)

            def attention(g, half, par, last_tail):
                copy_att2(g, half, par)
                for s in range(BH + 6):
                    if 0 <= s - 2 < BH:
                        exps(g, half, par, s - 2)
                    if 0 <= s - 3 < BH and (s - 3) % 2:
                        copy_pt(g, half, par, s - 3)
                    if s >= 13 and (s - 13) % BLOCK == 0:
                        copy_y1(g, (s - 13) // BLOCK)
                    if last_tail and s in (26, 27):
                        tail_yt(g - 1, s - 26)

            def body2(g, half, par):
                attention(g + 1, half, 1 - par, True)

            def finish2(g, half, par):
                tail_yt(g, 0)
                tail_yt(g, 1)

            groups(act, lambda: attention(0, 0, 0, False), body2, finish2)
            act.sem_inc(stage2_done, 1)

            def root3(g):
                act.wait_ge(var3, g + 1)
                nc.scalar.activation(ln3[:, 1, :], ln3[:, 0, :], ACT.Sqrt).then_inc(std3, 1)

            def copy_x3(g, par):
                act.wait_ge(x3_transposed, g + 1)
                nc.scalar.activation(xt3[par][:], ps[:, 0:2, :], ACT.Copy).then_inc(xt3_ready, 1)

            def silus(g, p):
                for m in range(2):
                    if m == 0:
                        act.wait_ge(dec_ready, PAR * g + p + 1)
                    else:
                        act.wait_ge(logit_full, WT * g + 2 * p + 2)
                    need(act, masked_ready, WT * g + 2 * (p - 2) + m + 1)
                    nc.scalar.activation(acts[p % 2][m][:], ps[:, 2 + m, :], ACT.Silu,
                                         bias=small[:, 8 + 2 * p + m:9 + 2 * p + m]).then_inc(acts_ready, 1)

            def first3():
                root3(0)
                copy_x3(0, 0)

            def body3(g, half, par):
                for p in range(PAR):
                    silus(g, p)
                    if p == 3:
                        root3(g + 1)
                    if p == 6:
                        copy_x3(g + 1, 1 - par)

            def last3(g, half, par):
                for p in range(PAR):
                    silus(g, p)

            groups(act, first3, body3, last3)

        @block.vector
        def _(dve):
            nc.vector.memset(ps[:, 6:8, :], 0.0).then_inc(psum_clear, 1)
            dve.wait_ge(consts, CONSTS)
            nc.vector.tensor_scalar(small[:, 6:8], small[:, 2:4], QK_SCALE, None, ALU.mult).then_inc(kb_ready, 1)

            def front1(g, half, par):
                dve.wait_ge(gathered[par], 32 * TILES * (half + 1))
                dve.wait_ge(lora_ready, g + 1)
                need(dve, h_stored[par], 16 * half)
                for m in range(2):
                    ins = nc.vector.scalar_tensor_tensor(
                        h_new[par][:, 2 * m:2 * m + 2, :], ps[:, 1 + m, :].rearrange("p (i c) -> p i c", i=2), LORA_SCALE,
                        staged[par][:, 2 * m:2 * m + 2, :], ALU.mult, ALU.add)
                ins.then_inc(h_made, 1)
                dve.wait_ge(h_made, g + 1)
                need(dve, x_transposed, g)
                layer_norm(dve, g, h_new[par], stats, mv, ln, xn, var_ready, std_ready, xn_ready, dve_chain)

            def back1(g, half, par, u0, u1):
                for u in range(u0, u1):
                    need(dve, qk_part2, 4 * g + u - 1)
                    dve.wait_ge(qk_part1, 4 * g + u + 1)
                    nc.vector.tensor_tensor(rest[u % 2][:], x32[u % 2][:], parts[u % 2][:, 0, :], ALU.subtract).then_inc(qk_rest, 1)
                    dve.wait_ge(qk_part2, 4 * g + u + 1)
                    nc.vector.tensor_tensor(parts[u % 2][:, 2, :], rest[u % 2][:], parts[u % 2][:, 1, :], ALU.subtract).then_inc(qk_part3, 1)

            def back1_v(g, half, par):
                for m in range(2):
                    dve.wait_ge(v_full, 2 * g + m + 1)
                    nc.vector.tensor_tensor(v_out[par][:, 2 * m:2 * m + 2, :], ps[:, 7, :].rearrange("p (i c) -> p i c", i=2),
                                            vb[:, :].unsqueeze(1).to_broadcast([P, 2, C]), ALU.add).then_inc(v_copied, 1)

            def body1(g, half, par):
                back1(g, half, par, 0, 2)
                front1(g + 1, half + par, 1 - par)
                back1_v(g, half, par)
                back1(g, half, par, 2, 4)
                need(dve, v_stored[1 - par], 16 * (half + par))

            def last1(g, half, par):
                back1(g, half, par, 0, 2)
                back1_v(g, half, par)
                back1(g, half, par, 2, 4)

            dve.wait_ge(w_loaded, 32)
            dve.wait_ge(psum_clear, 1)
            groups(dve, lambda: front1(0, 0, 0), body1, last1)

            dve.wait_ge(stage1_done, 1)
            dve.wait_ge(ek_loaded, 16)
            links = [LN_LINKS * G]

            def link(ins):
                links[0] += 1
                ins.then_inc(dve_chain, 1)
                dve.wait_ge(dve_chain, links[0])

            link(nc.vector.tensor_copy(ekp[:, 0, :], ek[:, 0, :]))
            link(nc.vector.tensor_tensor(ek[:, 1, :], ek[:, 0, :], ekp[:, 0, :], ALU.subtract))
            link(nc.vector.tensor_copy(ekp[:, 1, :], ek[:, 1, :]))
            nc.vector.tensor_tensor(ekp[:, 2, :], ek[:, 1, :], ekp[:, 1, :], ALU.subtract).then_inc(ek_split, 1)

            def add(g, half, par, x):
                dve.wait_ge(att1_full, BH * g + x + 1)
                if x == 0:
                    dve.wait_ge(att2_copied, A_USES * (g + 1))
                row = att[par][:, x, :]
                nc.vector.tensor_tensor(row, ps[:, x % 2, 0:SPAN], row, ALU.add).then_inc(scores_ready, 1)

            def maxima(g, half, par, x):
                dve.wait_ge(st_full, BH * g + x + 1)
                nc.vector.tensor_reduce(neg_max[:, x, :], ps[:, 2 + x % 2, 0:SPAN].rearrange("p (n s) -> p n s", n=3),
                                        AX.X, ALU.max, negate=True).then_inc(maxes, 1)
                dve.wait_ge(maxes, BH * g + x + 1)
                nc.vector.tensor_tensor(neg_max[:, x, 1:2], neg_max[:, x, 1:2], neg_max[:, x, 2:3], ALU.min).then_inc(max_ready, 1)

            def copy_pt(g, half, par, x):
                dve.wait_ge(pt_full, BH * g + x + 1)
                nc.vector.tensor_copy(att[par][:, x, :], ps[:, 4 + x % 2, 0:SPAN]).then_inc(pt_copied[0], 1)

            def copy_y2(g, c):
                dve.wait_ge(y2_full, 4 * g + c + 1)
                need(dve, y2_stored, 128 * g)
                nc.vector.tensor_copy(y2s[:, :, c * JC:(c + 1) * JC],
                                      ps[:, 7, :].rearrange("p (j x) -> p x j", x=BH)).then_inc(y2_copied, 1)

            def tail_norm(g, par, a):
                if a == 0:
                    flat = sums[par][:].rearrange("p h b j -> p (h b j)")
                    need(dve, h2_ready, g)
                    nc.vector.reciprocal(flat, flat).then_inc(inv_ready, 1)
                    dve.wait_ge(inv_ready, g + 1)
                dve.wait_ge(y_back, 2 * g + a + 1)
                for j in range(2):
                    ins = nc.vector.tensor_tensor(
                        yn[:, 2 * a + j, :].rearrange("p (h d) -> p h d", h=H),
                        ps[:, 7, j * C:(j + 1) * C].rearrange("p (h d) -> p h d", h=H),
                        sums[par][:, :, a, j:j + 1].to_broadcast([P, H, HD]), ALU.mult)
                ins.then_inc(yn_ready, 1)

            def tail_proj(g, a):
                dve.wait_ge(proj_full, 2 * g + a + 1)
                nc.vector.tensor_tensor(yn[:, 2 * a:2 * a + 2, :], ps[:, 7, :].rearrange("p (i c) -> p i c", i=2),
                                        bp[:, :].unsqueeze(1).to_broadcast([P, 2, C]), ALU.add).then_inc(proj_ready, 1)

            def attention(g, half, par, last_tail):
                for s in range(BH + 6):
                    if s < BH:
                        add(g, half, par, s)
                    if 0 <= s - 1 < BH:
                        maxima(g, half, par, s - 1)
                    if 0 <= s - 3 < BH and not (s - 3) % 2:
                        copy_pt(g, half, par, s - 3)
                    if last_tail:
                        if s in (4, 8, 12, 16):
                            copy_y2(g - 1, s // 4 - 1)
                        if s in (23, 24):
                            tail_norm(g - 1, 1 - par, s - 23)
                        if s in (29, 30):
                            tail_proj(g - 1, s - 29)

            def body2(g, half, par):
                attention(g + 1, half, 1 - par, True)

            def finish2(g, half, par):
                for c in range(4):
                    copy_y2(g, c)
                for a in range(2):
                    tail_norm(g, par, a)
                for a in range(2):
                    tail_proj(g, a)

            dve.wait_ge(w2_loaded, 48)
            groups(dve, lambda: attention(0, 0, 0, False), body2, finish2)
            dve.sem_inc(stage2_done, 1)

            dve.wait_ge(w3_loaded, 48)
            nc.vector.tensor_copy(tree[:], treef[:]).then_inc(tree_ready, 1)

            def front3(g, half, par):
                dve.wait_ge(h3_loaded[par], 16 * (half + 1))
                need(dve, x3_transposed, g)
                layer_norm(dve, g, h3[par], stats3, mv3, ln3, xn3, var3, std3, xn3_ready, chain3)

            def decide(g, p):
                dve.wait_ge(logit_full, WT * g + 2 * p + 1)
                need(dve, reach_full, WT * g + 2 * (p - 1))
                b = small[:, 8 + 2 * p:9 + 2 * p]
                nc.vector.tensor_scalar(dec[p % 2][:], ps[:, 2, :], b, 0.0, ALU.add, ALU.is_gt).then_inc(dec_ready, 1)

            def mask(g, p):
                for m in range(2):
                    dve.wait_ge(reach_full, WT * g + 2 * p + m + 1)
                    dve.wait_ge(acts_ready, WT * g + 2 * p + m + 1)
                    need(dve, ffn_full, PAR * g + p - 1)
                    nc.vector.scalar_tensor_tensor(masked[p % 2][m][:], ps[:, 4 + m, :], small[:, 24 + m:25 + m],
                                                   acts[p % 2][m][:], ALU.is_ge, ALU.mult).then_inc(masked_ready, 1)

            def finish(g, half, par):
                dve.wait_ge(ffn_full, PAR * (g + 1))
                for m in range(2):
                    ins = nc.vector.tensor_tensor(o3[par][:, 2 * m:2 * m + 2, :], ps[:, 6 + m, :].rearrange("p (i c) -> p i c", i=2),
                                                  h3[par][:, 2 * m:2 * m + 2, :], ALU.add)
                ins.then_inc(out_ready, 1)

            def trees(g, half, par, following):
                for p in range(PAR + 1):
                    if p < PAR:
                        decide(g, p)
                    if p >= 1:
                        mask(g, p - 1)
                    if p == 3 and following:
                        front3(g + 1, half + par, 1 - par)
                finish(g, half, par)
                if following:
                    need(dve, out_stored[1 - par], 16 * (half + par))

            groups(dve, lambda: front3(0, 0, 0), lambda g, half, par: trees(g, half, par, True),
                   lambda g, half, par: trees(g, half, par, False))

        @block.tensor
        def _(pe):
            pe.wait_ge(consts, CONSTS)
            pe.wait_ge(w_loaded, 32)

            def front1_lora(g, half, par):
                pe.wait_ge(gathered[par], 32 * TILES * (half + 1))
                need(pe, at_copied, g)
                for i in range(TILES):
                    ins = nc.tensor.transpose(ps[0:RANK, 0, i * P:(i + 1) * P], staged_a[par][:, i, :], ident[:])
                ins.then_inc(a_transposed, 1)
                pe.wait_ge(at_copied, g + 1)
                need(pe, h_made, g)
                for i in range(TILES):
                    ins = nc.tensor.matmul(ps[:, 1 + i // 2, (i % 2) * C:(i % 2 + 1) * C], at[:, i * P:(i + 1) * P],
                                           lb[:], start=True, stop=True)
                ins.then_inc(lora_ready, 1)

            def front1_x(g, half, par):
                pe.wait_ge(xn_ready, g + 1)
                need(pe, xt_ready, g)
                for m in range(CM):
                    for i in range(TILES):
                        ins = nc.tensor.transpose(ps[:, 3 + m, i * P:(i + 1) * P], xn[:, i, m * P:(m + 1) * P], ident[:])
                ins.then_inc(x_transposed, 1)

            def qk(g, half, par, u0, u1):
                pe.wait_ge(xt_ready, g + 1)
                for u in range(u0, u1):
                    need(pe, qk_copied, 4 * g + u - 1)
                    for m in range(CM):
                        ins = nc.tensor.matmul(ps[:, 5 + u % 2, :], wa[:, m, u * P:(u + 1) * P], xt[par][:, m, :],
                                               start=(m == 0), stop=(m == CM - 1))
                    ins.then_inc(qk_full, 1)

            def value(g, half, par, a0, a1):
                for a in range(a0, a1):
                    need(pe, v_copied, 2 * g + a)
                    for i in range(2):
                        for m in range(CM):
                            t = 2 * a + i
                            ins = nc.tensor.matmul(ps[:, 7, i * C:(i + 1) * C], xt[par][:, m, t * P:(t + 1) * P],
                                                   wa[:, m, 2 * C:3 * C], start=(m == 0), stop=(m == CM - 1))
                    ins.then_inc(v_full, 1)

            def first1():
                front1_lora(0, 0, 0)
                front1_x(0, 0, 0)

            def body1(g, half, par):
                qk(g, half, par, 0, 2)
                front1_lora(g + 1, half + par, 1 - par)
                value(g, half, par, 0, 1)
                front1_x(g + 1, half, 1 - par)
                value(g, half, par, 1, 2)
                qk(g, half, par, 2, 4)

            def last1(g, half, par):
                qk(g, half, par, 0, 2)
                value(g, half, par, 0, 2)
                qk(g, half, par, 2, 4)

            pe.wait_ge(psum_clear, 1)
            groups(pe, first1, body1, last1)

            def relative_keys(g, half, par):
                pe.wait_ge(q_loaded[par], 16 * len(Q_PARTS) * (half + 1))
                for n in range(A_USES):
                    if n < 2:
                        need(pe, scores_ready, BH * g)
                    else:
                        pe.wait_ge(att2_copied, A_USES * g + n - 1)
                    for j in range(JC):
                        col = n * JC + j
                        u = col if col < T else col - T
                        t = col if col < T else col - P
                        ins = nc.tensor.matmul(ps[:, n % 2, j * BH:(j + 1) * BH], r_stack[:, T - 1 - u:T - 1 - u + P],
                                               q_stack[par][:, :, t], start=True, stop=True)
                    ins.then_inc(att2_full, 1)

            def keys(g, half, par, x):
                if x == 0:
                    pe.wait_ge(k_loaded, 16 * len(K_PARTS) * (g + 1))
                if x < 2:
                    pe.wait_ge(att2_copied, A_USES * (g + 1))
                else:
                    pe.wait_ge(scores_ready, BH * g + x - 1)
                nc.tensor.matmul(ps[:, x % 2, 0:T], k_stack[:, x, 0:P], q_stack[par][0:KS, x, :], start=True, stop=True)
                nc.tensor.matmul(ps[:, x % 2, T:SPAN], k_stack[:, x, P:T], q_stack[par][0:KS, x, P:T],
                                 start=True, stop=True).then_inc(att1_full, 1)

            def to_rows(g, half, par, x):
                pe.wait_ge(scores_ready, BH * g + x + 1)
                need(pe, exp_done, BH * g + x - 1)
                for n in range(3):
                    ins = nc.tensor.transpose(ps[:, 2 + x % 2, n * P:(n + 1) * P], att[par][:, x, n * P:(n + 1) * P], ident[:])
                ins.then_inc(st_full, 1)

            def to_columns(g, half, par, x):
                pe.wait_ge(exp_done, BH * g + x + 1)
                need(pe, pt_copied[x % 2], BH // 2 * g + x // 2)
                for n in range(3):
                    ins = nc.tensor.transpose(ps[:, 4 + x % 2, n * P:(n + 1) * P], probs[x % 2][:, n * P:(n + 1) * P], ident[:])
                ins.then_inc(pt_full, 1)

            def values(g, half, par, x):
                h, b = x // GB, x % GB
                q = h % 4
                if x == 0:
                    pe.wait_ge(v_loaded[par], 16 * (half + 1))
                if x % BLOCK == 0:
                    need(pe, y1_copied, 4 * g + x // BLOCK)
                pe.wait_ge(pt_copied[x % 2], BH // 2 * g + x // 2 + 1)
                vh = v_in[par]
                nc.tensor.matmul(ps[32 * q:32 * q + HD, 6, b * T:(b + 1) * T], vh[:, 2 * b, h * HD:(h + 1) * HD],
                                 att[par][:, x, 0:T], start=(b == 0), stop=False, skip_group_check=True)
                ins = nc.tensor.matmul(ps[32 * q:32 * q + HD, 6, b * T + P:(b + 1) * T], vh[:, 2 * b + 1, h * HD:(h + 1) * HD],
                                       att[par][:, x, T:SPAN], start=False, stop=True, skip_group_check=True)
                if x % BLOCK == BLOCK - 1:
                    ins.then_inc(y1_full, 1)

            def relative_values(g, par, c, j0, j1):
                if j0 == 0:
                    if c == 0:
                        need(pe, proj_ready, 2 * g)
                    else:
                        pe.wait_ge(y2_copied, 4 * g + c)
                for j in range(j0, j1):
                    for q in range(4):
                        t = q * QT + c * JC + j
                        o = ps[32 * q:32 * q + HD, 7, j * BH:(j + 1) * BH]
                        ins = nc.tensor.matmul(o, rv[:, T - 1 - t, :], att[par][:, :, t], start=(j == 0), stop=(t < P),
                                               skip_group_check=True)
                        if t >= P:
                            ins = nc.tensor.matmul(o, rv[:, T - 1 - (t - P), :], att[par][:, :, t + P], start=False, stop=True,
                                                   skip_group_check=True)
                if j1 == JC:
                    ins.then_inc(y2_full, 1)

            def tail_back(g, a):
                if a == 0:
                    pe.wait_ge(y_summed, g + 1)
                    pe.wait_ge(y2_copied, 4 * (g + 1))
                else:
                    pe.wait_ge(yn_ready, 2 * g + 1)
                for j in range(2):
                    for m in range(CM):
                        t = 2 * a + j
                        ins = nc.tensor.transpose(ps[:, 7, j * C + m * P:j * C + (m + 1) * P], y1c[:, m, t * P:(t + 1) * P], ident[:])
                ins.then_inc(y_back, 1)

            def tail_yt(g, m):
                if m == 0:
                    pe.wait_ge(yn_ready, 2 * (g + 1))
                else:
                    pe.wait_ge(yt_copied, 2 * g + 1)
                for i in range(TILES):
                    ins = nc.tensor.transpose(ps[:, 7, i * P:(i + 1) * P], yn[:, i, m * P:(m + 1) * P], ident[:])
                ins.then_inc(yt_full, 1)

            def tail_proj(g, a):
                if a == 0:
                    pe.wait_ge(yt_copied, 2 * (g + 1))
                else:
                    pe.wait_ge(proj_ready, 2 * g + 1)
                for i in range(2):
                    for m in range(CM):
                        t = 2 * a + i
                        ins = nc.tensor.matmul(ps[:, 7, i * C:(i + 1) * C], yt[:, m, t * P:(t + 1) * P], wp[:, m, :],
                                               start=(m == 0), stop=(m == CM - 1))
                ins.then_inc(proj_full, 1)

            def attention(g, half, par, last_tail):
                relative_keys(g, half, par)
                for s in range(BH + 6):
                    if s < BH:
                        keys(g, half, par, s)
                    if 0 <= s - 1 < BH:
                        to_rows(g, half, par, s - 1)
                    if 0 <= s - 3 < BH:
                        to_columns(g, half, par, s - 3)
                    if 0 <= s - 5 < BH:
                        values(g, half, par, s - 5)
                    if last_tail:
                        if s < 16:
                            relative_values(g - 1, 1 - par, s // 4, s % 4 * 4, s % 4 * 4 + 4)
                        if s in (22, 23):
                            tail_back(g - 1, s - 22)
                        if s in (25, 26):
                            tail_yt(g - 1, s - 25)
                        if s in (28, 29):
                            tail_proj(g - 1, s - 28)

            def body2(g, half, par):
                attention(g + 1, half + par, 1 - par, True)

            def finish2(g, half, par):
                for c in range(4):
                    relative_values(g, par, c, 0, JC)
                for step in (tail_back, tail_yt, tail_proj):
                    step(g, 0)
                    step(g, 1)

            pe.wait_ge(stage1_done, 1)
            pe.wait_ge(v_copied, 2 * G)
            pe.wait_ge(w2_loaded, 48)
            pe.wait_ge(ones_ready, 5)
            pe.wait_ge(ek_stacked, 16 * len(K_PARTS))
            groups(pe, lambda: attention(0, 0, 0, False), body2, finish2)
            pe.wait_ge(proj_ready, 2 * G)
            pe.sem_inc(stage2_done, 1)

            def front3(g, half, par):
                pe.wait_ge(xn3_ready, g + 1)
                need(pe, xt3_ready, g)
                for m in range(CM):
                    for i in range(TILES):
                        ins = nc.tensor.transpose(ps[:, m, i * P:(i + 1) * P], xn3[:, i, m * P:(m + 1) * P], ident[:])
                ins.then_inc(x3_transposed, 1)

            def logits(g, par, p):
                for m in range(2):
                    need(pe, acts_ready, WT * g + 2 * (p - 1) + m + 1)
                    if m == 0:
                        need(pe, dec_ready, PAR * g + p)
                    w = (2 * p + m) * P
                    for k in range(CM):
                        ins = nc.tensor.matmul(ps[:, 2 + m, :], wi[:, k, w:w + P], xt3[par][:, k, :], start=(k == 0), stop=(k == CM - 1))
                    ins.then_inc(logit_full, 1)

            def reach(g, p):
                pe.wait_ge(dec_ready, PAR * g + p + 1)
                for m in range(2):
                    need(pe, masked_ready, WT * g + 2 * (p - 1) + m + 1)
                    nc.tensor.matmul(ps[:, 4 + m, :], tree[:, m * P:(m + 1) * P], dec[p % 2][:], start=True, stop=True).then_inc(reach_full, 1)

            def combine(g, p):
                for m in range(2):
                    pe.wait_ge(masked_ready, WT * g + 2 * p + m + 1)
                    if p == 0 and m == 0:
                        need(pe, out_ready, g)
                    for i in range(TILES):
                        ins = nc.tensor.matmul(ps[:, 6 + i // 2, (i % 2) * C:(i % 2 + 1) * C], masked[p % 2][m][:, i * P:(i + 1) * P],
                                               wo[:, 2 * p + m, :], start=(p == 0 and m == 0 and i % 2 == 0),
                                               stop=(p == PAR - 1 and m == 1), skip_group_check=True)
                ins.then_inc(ffn_full, 1)

            def trees(g, half, par, following):
                pe.wait_ge(xt3_ready, g + 1)
                for p in range(PAR + 2):
                    if p < PAR:
                        logits(g, par, p)
                    if 1 <= p <= PAR:
                        reach(g, p - 1)
                    if p >= 2:
                        combine(g, p - 2)
                    if p == 6 and following:
                        front3(g + 1, half, 1 - par)

            pe.wait_ge(w3_loaded, 48)
            pe.wait_ge(tree_ready, 1)
            groups(pe, lambda: front3(0, 0, 0), lambda g, half, par: trees(g, half, par, True),
                   lambda g, half, par: trees(g, half, par, False))


def tree_constants():
    tree, turns = np.zeros((P, 2 * P), np.float32), np.zeros((2 * P,), np.float32)
    for n in range(2 ** (DEPTH + 1) - 1):
        col = n if n < P - 1 else n + 1
        at = n
        while at:
            up, right = (at - 1) // 2, at % 2 == 0
            tree[up, col] = 1.0 if right else -1.0
            turns[col] += right
            at = up
    return tree, np.ascontiguousarray((turns - 0.5).reshape(2, P).T)


def kernel(x, L0_tok_weight, L0_tok_lora_A, L0_tok_lora_B, L0_attn_Wattn, L0_attn_battn, L0_attn_Wproj,
           L0_attn_bproj, L0_attn_embk, L0_attn_embv, L0_ffn_W_in, L0_ffn_b_in, L0_ffn_W_out):
    import concourse.bacc as bacc
    from concourse.bass_utils import run_bass_kernel_spmd

    def by_tile(a):
        a = a.reshape(PAR, 2 * P - 1, -1)
        gap = np.zeros((PAR, 1, a.shape[2]), a.dtype)
        return np.concatenate([a[:, :P - 1], gap, a[:, P - 1:]], axis=1).reshape(WT * P, -1)

    x = np.asarray(x)
    tree, thresholds = tree_constants()
    embv = np.asarray(L0_attn_embv)
    arrays = {
        "idx": x.reshape(TOK // P, P).T,
        "tok_w": L0_tok_weight,
        "lora_a": L0_tok_lora_A,
        "lora_b": L0_tok_lora_B,
        "wattn": L0_attn_Wattn,
        "battn": np.asarray(L0_attn_battn).reshape(6, P).T,
        "vbias": np.asarray(L0_attn_battn)[2 * C:].reshape(1, C),
        "wproj": L0_attn_Wproj,
        "bproj": np.asarray(L0_attn_bproj).reshape(1, C),
        "embk_rev": np.asarray(L0_attn_embk)[::-1].T,
        "embv_pad": np.concatenate([embv[::-1], np.zeros((P - 1, HD), embv.dtype)]),
        "w_in": by_tile(np.asarray(L0_ffn_W_in)).T,
        "b_in": by_tile(np.asarray(L0_ffn_b_in)).reshape(WT, P).T,
        "w_out": by_tile(np.asarray(L0_ffn_W_out).T),
        "ident_in": np.eye(P, dtype=np.float32),
        "tree_in": tree,
        "thr_in": thresholds,
    }
    arrays = {k: np.ascontiguousarray(v) for k, v in arrays.items()}
    nc = bacc.Bacc("TRN2", target_bir_lowering=False, num_devices=1)
    args = [nc.dram_tensor(k, v.shape, mybir.dt.from_np(v.dtype), kind="ExternalInput").ap() for k, v in arrays.items()]
    out = nc.dram_tensor("out", (TOK, C), F32, kind="ExternalOutput").ap()
    tower_kernel(nc, *args, out)
    r = run_bass_kernel_spmd(nc, [arrays], core_ids=[0])
    return r.results[0]["out"].reshape(BATCH, T, C)
```

```python
import math
import numpy as np
import concourse.bass as bass
from concourse import mybir
from contextlib import ExitStack

F32 = mybir.dt.float32
BF16 = mybir.dt.bfloat16
F32R = mybir.dt.float32r
U32 = mybir.dt.uint32
ALU = mybir.AluOpType
ACT = mybir.ActivationFunctionType
AX = mybir.AxisListType

P = 128
BATCH, T, C, H = 16, 256, 256, 16
HD = C // H
TOK = BATCH * T
G = 8
GT = TOK // G
TILES = GT // P
GB = GT // T
BH = GB * H
CM = C // P
RANK = 8
LORA_SCALE = 8 / math.sqrt(RANK)
QK_SCALE = 1 / math.sqrt(HD)
EPS = 1e-5
PAR, DEPTH = 8, 7
WT = 2 * PAR
Q_PARTS = (0, 0, 1, 1, 0, 2)
K_PARTS = (0, 1, 0, 1, 2, 0)
KS = len(Q_PARTS) * HD
MASK = -1e30
SPAN = T + P
BLOCK = 8
JC = 16
QT = T // 4


def need(eng, sem, count):
    if not (isinstance(count, int) and count <= 0):
        eng.wait_ge(sem, count)


def apart(eng, waits_done):
    eng.sem_inc(waits_done, 1)


def deep_groups(eng, prologue, body):
    prologue()
    body(0, 0, 0)
    body(1, 0, 1)
    with eng.Fori(0, 2) as i:
        body(i * 2 + 2, i + 1, 0)
        body(i * 2 + 3, i + 1, 1)
    body(6, 3, 0)
    body(7, 3, 1)


def beyond(g):
    return isinstance(g, int) and g >= G


def last(g):
    return isinstance(g, int) and g == G - 1


def first(g):
    return isinstance(g, int) and g == 0


def groups(eng, prologue, body, epilogue):
    prologue()
    body(0, 0, 0)
    with eng.Fori(0, 3) as i:
        body(i * 2 + 1, i, 1)
        body(i * 2 + 2, i + 1, 0)
    epilogue(G - 1, G // 2 - 1, 1)


def tower_kernel(nc, idx, tok_w, lora_a, lora_b, wattn, battn, vbias, wproj, bproj, embk_rev, embv_pad,
                 w_in, b_in, w_out, ident_in, tree_in, thr_in, out):
    ctx = ExitStack()
    with ctx:
        def sb(name, shape, dt=F32):
            return ctx.enter_context(nc.sbuf_tensor(name, shape, dt))

        def sem(name):
            return ctx.enter_context(nc.semaphore(name))

        def two(name):
            return [sem(f"{name}{n}") for n in range(2)]

        h_d = nc.dram_tensor("h_d", (TOK, C), F32, kind="Internal").ap()
        h2_d = nc.dram_tensor("h2_d", (TOK, C), F32, kind="Internal").ap()
        v_d = nc.dram_tensor("v_d", (TOK, C), F32, kind="Internal").ap()
        qk_d = nc.dram_tensor("qk_d", (2, 3, C, TOK), BF16, kind="Internal").ap()
        y1_d = nc.dram_tensor("y1_d", (C, TOK), F32, kind="Internal").ap()
        y2_d = nc.dram_tensor("y2_d", (C, TOK), F32, kind="Internal").ap()

        ps = ctx.enter_context(nc.psum_tensor("ps", [P, 8, 512], F32))

        def rows(dram, g):
            return dram[bass.ds(g * GT, GT), :].rearrange("(i p) c -> p i c", p=P)

        ident = sb("ident", [P, P])
        small = sb("small", [P, 32])
        consts = sem("consts")
        kb_ready = sem("kb_ready")
        psum_clear = sem("psum_clear")
        CONSTS = 16 * 5

        sp_waited, pool_waited, dve_waited = sem("sp_waited"), sem("pool_waited"), sem("dve_waited")

        idx_sb = sb("idx_sb", [P, TOK // P], mybir.dt.int32)
        idx_g = [sb(f"idx_g{n}", [P, TILES], mybir.dt.int32) for n in range(2)]
        idx_loaded, idx_ready = sem("idx_loaded"), sem("idx_ready")

        stage1 = ExitStack()

        def sb1(name, shape, dt=F32):
            return stage1.enter_context(nc.sbuf_tensor(name, shape, dt))

        w_loaded = sem("w_loaded")
        gathered = two("gathered")
        a_transposed, at_copied, lora_ready, h_made = (sem(n) for n in ("a_transposed", "at_copied", "lora_ready", "h_made"))
        var_ready, std_ready, xn_ready, x_transposed, xt_ready = (sem(n) for n in ("var_ready", "std_ready", "xn_ready", "x_transposed", "xt_ready"))
        qk_full, qk_copied, qk_rest, qk_part2, qk_part3 = (sem(n) for n in ("qk_full", "qk_copied", "qk_rest", "qk_part2", "qk_part3"))
        v_full, v_copied, wa_rounded, wa_split, xt_rounded = (sem(n) for n in ("v_full", "v_copied", "wa_rounded", "wa_split", "xt_rounded"))
        h_stored, v_stored, parts_stored = two("h_stored"), two("v_stored"), two("parts_stored")
        dve_chain, ek_chain = sem("dve_chain"), sem("ek_chain")

        wa = sb1("wa", [P, CM, 3 * C])
        vb = sb1("vb", [P, C])
        lb = sb1("lb", [RANK, C])
        staged = [sb1(f"staged{n}", [P, TILES, C]) for n in range(2)]
        staged_a = [sb1(f"staged_a{n}", [P, TILES, RANK]) for n in range(2)]
        at = sb1("at", [RANK, GT])
        h_new = [sb1(f"h_new{n}", [P, TILES, C]) for n in range(2)]
        stats = sb1("stats", [P, TILES, 6])
        mv = sb1("mv", [P, TILES, 2])
        ln = sb1("ln", [P, 4, TILES])
        xn = sb1("xn", [P, TILES, C])
        wa_hi, wa_lo = sb1("wa_hi", [P, CM, 3 * C], F32R), sb1("wa_lo", [P, CM, 3 * C], F32R)
        xt_hi = [sb1(f"xt_hi{n}", [P, CM, GT], F32R) for n in range(2)]
        xt_lo = [sb1(f"xt_lo{n}", [P, CM, GT], F32R) for n in range(2)]
        x32 = [sb1(f"x32_{n}", [P, GT]) for n in range(2)]
        rest = [sb1(f"rest{n}", [P, GT]) for n in range(2)]
        parts = [sb1(f"parts{n}", [P, 3, GT], BF16) for n in range(2)]
        v_out = [sb1(f"v_out{n}", [P, TILES, C]) for n in range(2)]
        STAGE1_STORES = None
        stage1_stored = [(h_stored, 16 * G // 2), (v_stored, 16 * G // 2), (parts_stored, 16 * 2 * G)]
        LN_LINKS = 7

        def layer_norm(dve, call, src, st, mvt, lnt, dst, variance, std, done, chain):
            n = [call * LN_LINKS]

            def link(ins):
                n[0] = n[0] + 1
                ins.then_inc(chain, 1)
                dve.wait_ge(chain, n[0])

            for i in range(TILES):
                ins = nc.vector.bn_stats(st[:, i, :], src[:, i, :])
            link(ins)
            apart(dve, dve_waited)
            for i in range(TILES):
                ins = nc.vector.bn_aggr(mvt[:, i, :], st[:, i, :])
            link(ins)
            nc.vector.tensor_scalar(lnt[:, 0, :], mvt[:, :, 1], EPS, None, ALU.add).then_inc(variance, 1)
            dve.wait_ge(std, call + 1)
            link(nc.vector.reciprocal(lnt[:, 2, :], lnt[:, 1, :]))
            link(nc.vector.tensor_tensor(lnt[:, 3, :], lnt[:, 2, :], lnt[:, 2, :], ALU.mult))
            link(nc.vector.tensor_tensor(lnt[:, 3, :], lnt[:, 3, :], lnt[:, 0, :], ALU.mult))
            link(nc.vector.tensor_scalar(lnt[:, 3, :], lnt[:, 3, :], -0.5, 1.5, ALU.mult, ALU.add))
            link(nc.vector.tensor_tensor(lnt[:, 2, :], lnt[:, 2, :], lnt[:, 3, :], ALU.mult))
            for i in range(TILES):
                ins = nc.vector.tensor_scalar(dst[:, i, :], src[:, i, :], mvt[:, i, 0:1], lnt[:, 2, i:i + 1],
                                              ALU.subtract, ALU.mult)
            link_last = ins
            link_last.then_inc(done, 1)

        stage1.close()
        stage2 = ExitStack()

        def sb2(name, shape, dt=F32):
            return stage2.enter_context(nc.sbuf_tensor(name, shape, dt))

        stage1_done = sem("stage1_done")
        att = [sb2(f"att{n}", [P, BH, SPAN]) for n in range(2)]
        q_stack = [sb2(f"q_stack{n}", [KS + 1, BH, T], BF16) for n in range(2)]
        k_stack = sb2("k_stack", [KS, BH, T], BF16)
        r_stack = sb2("r_stack", [KS + 1, SPAN], BF16)
        ekp = sb2("ekp", [HD, 3, T], BF16)
        rv = sb2("rv", [P, T, HD])
        wp = sb2("wp", [P, CM, C])
        bp = sb2("bp", [P, C])
        v_in = [sb2(f"v_in{n}", [P, TILES, C]) for n in range(2)]
        neg_max = sb2("neg_max", [P, BH, 3])
        sums = [sb2(f"sums{n}", [P, H, GB, 2]) for n in range(2)]
        probs = [sb2(f"probs{n}", [P, SPAN]) for n in range(2)]
        y1s = sb2("y1s", [P, H // 4, GT])
        y2s = sb2("y2s", [P, BH, QT])
        ek = y1s[0:HD, 0, :].rearrange("d (n t) -> d n t", n=2)
        y1c = sb2("y1c", [P, CM, GT])
        y2c = sb2("y2c", [P, CM, GT])
        yn = sb2("yn", [P, TILES, C])
        yt = y2c
        hin = y1c[:, :, :].rearrange("p m t -> p (m t)").rearrange("p (i c) -> p i c", i=TILES)

        w2_loaded, ek_loaded, ek_split, ek_stacked = sem("w2_loaded"), sem("ek_loaded"), sem("ek_split"), sem("ek_stacked")
        ones_ready = sem("ones_ready")
        q_loaded, v_loaded = two("q_loaded"), two("v_loaded")
        k_loaded, h_loaded = two("k_loaded"), sem("h_loaded")
        att2_full, att2_copied, att1_full, scores_ready = (sem(n) for n in ("att2_full", "att2_copied", "att1_full", "scores_ready"))
        st_full, maxes, max_ready, exp_done, pt_full = (sem(n) for n in ("st_full", "maxes", "max_ready", "exp_done", "pt_full"))
        pt_copied = two("pt_copied")
        y1_full, y1_copied, y1_stored, y2_full, y2_copied, y2_stored = (sem(n) for n in ("y1_full", "y1_copied", "y1_stored", "y2_full", "y2_copied", "y2_stored"))
        yc_loaded, y_summed, inv_ready = sem("yc_loaded"), sem("y_summed"), sem("inv_ready")
        y_back, yn_ready, yt_full, yt_copied, proj_full, proj_ready, h2_ready, h2_stored = (
            sem(n) for n in ("y_back", "yn_ready", "yt_full", "yt_copied", "proj_full", "proj_ready", "h2_ready", "h2_stored"))
        A_USES = SPAN // JC
        STEPS = BH + 6
        A_AT = {}
        for n in range(A_USES):
            A_AT.setdefault(16 + n * (STEPS - 17) // A_USES, []).append(n)
        BACK_AT, YT_PE_AT, YT_AT, PROJ_AT = (24, 26), (28, 30), (29, 31), (32, 34)

        stage2.close()
        stage3 = ExitStack()

        def sb3(name, shape, dt=F32):
            return stage3.enter_context(nc.sbuf_tensor(name, shape, dt))

        wi = sb3("wi", [P, CM, WT * P])
        wo = sb3("wo", [P, WT, C])
        wo_lo = sb3("wo_lo", [P, WT, C], F32R)
        h3 = [sb3(f"h3_{n}", [P, TILES, C]) for n in range(2)]
        treef = sb3("treef", [P, 2 * P])
        tree = sb3("tree", [P, 2 * P], BF16)
        stats3 = sb3("stats3", [P, TILES, 6])
        mv3 = sb3("mv3", [P, TILES, 2])
        ln3 = sb3("ln3", [P, 4, TILES])
        xn3 = sb3("xn3", [P, TILES, C])
        x_hi = [sb3(f"x_hi{n}", [P, CM, GT], F32R) for n in range(2)]
        x_lo = [sb3(f"x_lo{n}", [P, CM, GT], F32R) for n in range(2)]
        o3 = [sb3(f"o3_{n}", [P, TILES, C]) for n in range(2)]
        acts = [[sb3(f"acts{n}{m}", [P, GT]) for m in range(2)] for n in range(2)]
        dec = [sb3(f"dec{n}", [P, GT], BF16) for n in range(2)]
        used = 4 * (2 * TILES * C + 2 * P + TILES * 12 + TILES * C + 4 * CM * GT + 2 * TILES * C + 4 * GT) + 2 * (2 * P + 2 * GT)
        sb3("gap3", [P, BH * SPAN - used // 4])
        wi_hi = sb3("wi_hi", [P, CM, WT * P], F32R)
        wi_lo = sb3("wi_lo", [P, CM, WT * P], F32R)
        wo_hi = sb3("wo_hi", [P, WT, C], F32R)
        masked = [[sb3(f"masked{n}{m}", [P, GT]) for m in range(2)] for n in range(2)]
        m_hi = [[sb3(f"m_hi{n}{m}", [P, GT], F32R) for m in range(2)] for n in range(2)]
        m_lo = [[sb3(f"m_lo{n}{m}", [P, GT], F32R) for m in range(2)] for n in range(2)]
        stage3.close()
        w3_loaded, tree_loaded, tree_ready, w_hi, w_split = (sem(n) for n in ("w3_loaded", "tree_loaded", "tree_ready", "w_hi", "w_split"))
        x_rounded, hi_ready, lo_ready = (sem(n) for n in ("x_rounded", "hi_ready", "lo_ready"))
        h3_loaded, out_stored = two("h3_loaded"), two("out_stored")
        var3, std3, xn3_ready, x3_transposed, xt3_ready = (sem(n) for n in ("var3", "std3", "xn3_ready", "x3_transposed", "xt3_ready"))
        logit_full, dec_ready, acts_ready, reach_full, masked_ready, ffn_full, out_ready = (
            sem(n) for n in ("logit_full", "dec_ready", "acts_ready", "reach_full", "masked_ready", "ffn_full", "out_ready"))
        chain3 = sem("chain3")

        block = ctx.enter_context(nc.Block())

        @block.sync
        def _(sp):
            sp.dma_start(idx_sb[:], idx).then_inc(idx_loaded, 16)
            sp.dma_start(ident[:], ident_in).then_inc(consts, 16)
            sp.dma_start(small[:, 0:6], battn).then_inc(consts, 16)
            sp.dma_start(small[:, 8:8 + WT], b_in).then_inc(consts, 16)
            sp.dma_start(small[:, 24:26], thr_in).then_inc(consts, 16)
            sp.dma_start(lb[:], lora_b).then_inc(consts, 16)
            sp.dma_start(wa[:], wattn.rearrange("(m p) n -> p m n", p=P)).then_inc(w_loaded, 16)
            sp.dma_start(vb[:], vbias.to_broadcast([P, C])).then_inc(w_loaded, 16)

            def store_h(g, half, par):
                sp.wait_ge(h_made, g + 1)
                apart(sp, sp_waited)
                sp.dma_start(rows(h_d, g), h_new[par][:]).then_inc(h_stored[par], 16)

            def store_qkv(g, half, par):
                for u in range(4):
                    sp.wait_ge(qk_part3, 4 * g + u + 1)
                    apart(sp, sp_waited)
                    dst = qk_d[u // 2, :, (u % 2) * P:(u % 2 + 1) * P, bass.ds(g * GT, GT)]
                    sp.dma_start(dst.rearrange("n p t -> p n t"), parts[u % 2][:]).then_inc(parts_stored[u % 2], 16)
                sp.wait_ge(v_copied, 2 * (g + 1))
                apart(sp, sp_waited)
                sp.dma_start(rows(v_d, g), v_out[par][:]).then_inc(v_stored[par], 16)

            def body1(g, half, par):
                if not beyond(g + 2):
                    store_h(g + 2, half + 1, par)
                if last(g):
                    load_first()
                store_qkv(g, half, par)

            def load_q(g, par):
                need(sp, y1_full, 4 * (g - 1))
                for n, p in enumerate(Q_PARTS):
                    src = qk_d[0, p, :, bass.ds(g * GT, GT)].rearrange("(h d) t -> d h t", d=HD)
                    dst = q_stack[par][n * HD:(n + 1) * HD, :, :]
                    sp.dma_start(dst.rearrange("d (h b) t -> d h (b t)", h=H), src).then_inc(q_loaded[par], 16)
                sp.dma_start(v_in[par][:], rows(v_d, g)).then_inc(v_loaded[par], 16)

            def load_k(g, part):
                if not first(g):
                    sp.wait_ge(att1_full, BH * (g - 1) + BH // 2 * (part + 1))
                    apart(sp, sp_waited)
                for n, p in enumerate(K_PARTS):
                    src = qk_d[1, p, part * C // 2:(part + 1) * C // 2, bass.ds(g * GT, GT)].rearrange("(h d) t -> d h t", d=HD)
                    dst = k_stack[n * HD:(n + 1) * HD, part * BH // 2:(part + 1) * BH // 2, :]
                    sp.dma_start(dst.rearrange("d (h b) t -> d h (b t)", h=H // 2), src).then_inc(k_loaded[part], 16)

            def load_first():
                sp.wait_ge(parts_stored[0], 32)
                sp.wait_ge(parts_stored[1], 32)
                sp.wait_ge(v_stored[0], 16)
                load_q(0, 0)
                load_k(0, 0)
                load_k(0, 1)
                sp.wait_ge(ek_split, 1)
                for n, part in enumerate(K_PARTS):
                    sp.dma_start(r_stack[n * HD:(n + 1) * HD, 0:T], ekp[:, part, :]).then_inc(ek_stacked, 16)

            def first1():
                store_h(0, 0, 0)
                store_h(1, 0, 1)

            sp.dma_start(ek[:, 0, :], embk_rev).then_inc(ek_loaded, 16)
            sp.dma_start(rv[:], bass.AP(embv_pad.tensor, 0, [[HD, P], [HD, T], [1, HD]])).then_inc(w2_loaded, 16)
            sp.dma_start(wp[:], wproj.rearrange("(m p) n -> p m n", p=P)).then_inc(w2_loaded, 16)
            sp.dma_start(bp[:], bproj.to_broadcast([P, C])).then_inc(w2_loaded, 16)
            deep_groups(sp, first1, body1)
            for pair, count in stage1_stored:
                for s in pair:
                    sp.wait_ge(s, count)
            sp.sem_inc(stage1_done, 1)

            def store_y(g):
                sp.wait_ge(y1_copied, 4 * (g + 1))
                apart(sp, sp_waited)
                for q in range(4):
                    dst = y1_d.rearrange("(a q d) t -> q d a t", q=4, d=HD)[q][:, :, bass.ds(g * GT, GT)]
                    sp.dma_start(dst, y1s[32 * q:32 * q + HD, :, :]).then_inc(y1_stored, 16)
                sp.wait_ge(y2_copied, 4 * (g + 1))
                apart(sp, sp_waited)
                for q in range(4):
                    for b in range(GB):
                        dst = y2_d.rearrange("(h d) t -> d h t", d=HD)[:, :, bass.ds(g * GT + b * T + q * QT, QT)]
                        src = y2s[32 * q:32 * q + HD, :, :].rearrange("p (h b) t -> p b h t", b=GB)[:, b]
                        sp.dma_start(dst, src).then_inc(y2_stored, 16)
                sp.wait_ge(y1_stored, 64 * (g + 1))
                apart(sp, sp_waited)
                need(sp, h2_stored, 16 * g)
                apart(sp, sp_waited)
                sp.dma_start(y1c[:], y1_d[:, bass.ds(g * GT, GT)].rearrange("(m p) t -> p m t", p=P)).then_inc(yc_loaded, 16)
                sp.wait_ge(y2_stored, 128 * (g + 1))
                apart(sp, sp_waited)
                sp.dma_start(y2c[:], y2_d[:, bass.ds(g * GT, GT)].rearrange("(m p) t -> p m t", p=P)).then_inc(yc_loaded, 16)

            def load_h1(g):
                sp.wait_ge(y_back, 2 * (g + 1))
                apart(sp, sp_waited)
                sp.dma_start(hin, rows(h_d, g)).then_inc(h_loaded, 16)

            def load_h(g, par):
                need(sp, out_ready, g - 1)
                apart(sp, sp_waited)
                sp.dma_start(h3[par][:], rows(h2_d, g)).then_inc(h3_loaded[par], 16)

            def store_h2(g):
                sp.wait_ge(h2_ready, g + 1)
                apart(sp, sp_waited)
                sp.dma_start(rows(h2_d, g), hin).then_inc(h2_stored, 16)

            def body2(g, half, par):
                load_q(g + 1, 1 - par)
                if not first(g):
                    store_y(g - 1)
                load_k(g + 1, 0)
                if not first(g):
                    load_h1(g - 1)
                    store_h2(g - 1)
                load_k(g + 1, 1)

            def last2(g, half, par):
                store_y(g - 1)
                load_h1(g - 1)
                store_h2(g - 1)
                sp.wait_ge(y2_full, 4 * (G - 1))
                sp.dma_start(wi[:], w_in.rearrange("(m p) n -> p m n", p=P)).then_inc(w3_loaded, 16)
                sp.dma_start(wo[:], w_out.rearrange("(m p) n -> p m n", p=P)).then_inc(w3_loaded, 16)
                store_y(g)
                load_h1(g)
                sp.dma_start(treef[:], tree_in).then_inc(tree_loaded, 16)
                load_h(0, 0)
                store_h2(g)

            groups(sp, lambda: None, body2, last2)
            sp.wait_ge(h2_stored, 16 * G)

            def store(g, half, par):
                sp.wait_ge(out_ready, g + 1)
                apart(sp, sp_waited)
                sp.dma_start(rows(out, g), o3[par][:]).then_inc(out_stored[par], 16)

            def body3(g, half, par):
                load_h(g + 1, 1 - par)
                store(g, half, par)

            groups(sp, lambda: None, body3, store)
            for s in out_stored:
                sp.wait_ge(s, 16 * G // 2)

        @block.gpsimd
        def _(pool):
            for n in range(2):
                nc.gpsimd.memset(q_stack[n][KS:KS + 1, :, :], 1.0).then_inc(ones_ready, 1)
            nc.gpsimd.memset(r_stack[0:KS, T:SPAN], 0.0).then_inc(ones_ready, 1)
            nc.gpsimd.memset(r_stack[KS:KS + 1, 0:T], 0.0).then_inc(ones_ready, 1)
            nc.gpsimd.memset(r_stack[KS:KS + 1, T:SPAN], MASK).then_inc(ones_ready, 1)
            pool.wait_ge(ones_ready, 5)
            pool.wait_ge(idx_loaded, 16)

            def gather(g, half, par):
                need(pool, h_made, g - 1)
                apart(pool, pool_waited)
                nc.gpsimd.tensor_copy(idx_g[par][:], idx_sb[:, bass.ds(g * TILES, TILES)]).then_inc(idx_ready, 1)
                pool.wait_ge(idx_ready, g + 1)
                apart(pool, pool_waited)
                for i in range(TILES):
                    off = bass.IndirectOffsetOnAxis(ap=idx_g[par][:, i:i + 1].bitcast(U32), axis=0)
                    pool.indirect_dma_start(staged[par][:, i, :], None, tok_w, off).then_inc(gathered[par], 16)
                    pool.indirect_dma_start(staged_a[par][:, i, :], None, lora_a, off).then_inc(gathered[par], 16)

            gather(0, 0, 0)
            gather(1, 0, 1)
            with pool.Fori(0, 3) as i:
                gather(i * 2 + 2, i + 1, 0)
                gather(i * 2 + 3, i + 1, 1)

            def tail(g):
                pool.wait_ge(yc_loaded, 32 * (g + 1))
                nc.gpsimd.tensor_tensor(y1c[:], y1c[:], y2c[:], ALU.add).then_inc(y_summed, 1)
                pool.wait_ge(h_loaded, 16 * (g + 1))
                pool.wait_ge(proj_ready, 2 * (g + 1))
                nc.gpsimd.tensor_tensor(hin, hin, yn[:], ALU.add).then_inc(h2_ready, 1)

            tail(0)
            with pool.Fori(0, 3) as i:
                tail(i * 2 + 1)
                tail(i * 2 + 2)
            tail(G - 1)

        @block.scalar
        def _(act):
            def copy_at(g):
                act.wait_ge(a_transposed, g + 1)
                nc.scalar.activation(at[:], ps[0:RANK, 0, :], ACT.Copy).then_inc(at_copied, 1)

            def root1(g):
                act.wait_ge(var_ready, g + 1)
                nc.scalar.activation(ln[:, 1, :], ln[:, 0, :], ACT.Sqrt).then_inc(std_ready, 1)

            def round_xt(g, par):
                act.wait_ge(x_transposed, g + 1)
                nc.scalar.activation(xt_hi[par][:], ps[:, 3:5, :], ACT.Copy).then_inc(xt_rounded, 1)

            def back1(g, u0, u1):
                for u in range(u0, u1):
                    act.wait_ge(qk_full, 4 * g + u + 1)
                    need(act, qk_part3, 4 * g + u - 1)
                    need(act, parts_stored[u % 2], 16 * (2 * g + u // 2))
                    bias = small[:, u:u + 1] if u < 2 else small[:, 4 + u:5 + u]
                    for dst in (x32[u % 2][:], parts[u % 2][:, 0, :]):
                        ins = nc.scalar.activation(dst, ps[:, 5 + u % 2, :], ACT.Identity, bias=bias,
                                                   scale=1.0 if u < 2 else QK_SCALE)
                    ins.then_inc(qk_copied, 1)

            def first1():
                copy_at(0)
                root1(0)
                copy_at(1)
                round_xt(0, 0)
                root1(1)

            def body1(g, half, par):
                if not beyond(g + 1):
                    round_xt(g + 1, 1 - par)
                if not beyond(g + 2):
                    copy_at(g + 2)
                back1(g, 0, 2)
                if not beyond(g + 2):
                    root1(g + 2)
                back1(g, 2, 4)

            act.wait_ge(consts, CONSTS)
            act.wait_ge(kb_ready, 1)
            act.wait_ge(w_loaded, 32)
            nc.scalar.activation(wa_hi[:], wa[:], ACT.Copy).then_inc(wa_rounded, 1)
            deep_groups(act, first1, body1)

            act.wait_ge(stage1_done, 1)

            def copy_att2(g, half, par, n):
                if n == 0:
                    need(act, y2_full, 4 * (g - 1))
                act.wait_ge(att2_full, A_USES * g + n + 1)
                nc.scalar.activation(att[par][:, :, n * JC:(n + 1) * JC],
                                     ps[:, 1, :].rearrange("p (j x) -> p x j", x=BH), ACT.Copy).then_inc(att2_copied, 1)

            def exps(g, half, par, x):
                act.wait_ge(max_ready, BH * g + x + 1)
                need(act, pt_full, BH * g + x - 1)
                sc, pr = ps[:, 2 + x % 2, :], probs[x % 2]
                h, b = x // GB, x % GB
                nc.scalar.activation(pr[:, 0:P], sc[:, 0:P], ACT.Exp, bias=neg_max[:, x, 0:1],
                                     accum_out=sums[par][:, h, b, 0:1])
                nc.scalar.activation(pr[:, P:SPAN], sc[:, P:SPAN], ACT.Exp, bias=neg_max[:, x, 1:2],
                                     accum_out=sums[par][:, h, b, 1:2]).then_inc(exp_done, 1)

            def copy_pt(g, half, par, x):
                act.wait_ge(pt_full, BH * g + x + 1)
                nc.scalar.activation(att[par][:, x, :], ps[:, 4 + x % 2, 0:SPAN], ACT.Copy).then_inc(pt_copied[0], 1)

            def copy_y1(g, nb):
                act.wait_ge(y1_full, 4 * g + nb + 1)
                need(act, y1_stored, 64 * g)
                nc.scalar.activation(y1s[:, nb, :], ps[:, 6, :], ACT.Copy).then_inc(y1_copied, 1)

            def tail_yt(g, m):
                act.wait_ge(yt_full, 2 * g + m + 1)
                nc.scalar.activation(yt[:, m, :], ps[:, 7, :], ACT.Copy).then_inc(yt_copied, 1)

            def attention(g, half, par, following):
                for s in range(STEPS):
                    if s >= 13 and (s - 13) % BLOCK == 0:
                        copy_y1(g, (s - 13) // BLOCK)
                    if 0 <= s - 2 < BH:
                        exps(g, half, par, s - 2)
                    if 0 <= s - 3 < BH // 2:
                        copy_pt(g, half, par, s - 3)
                    if following:
                        for n in A_AT.get(s, ()):
                            copy_att2(g + 1, half + par, 1 - par, n)
                    if not first(g) and s in YT_AT:
                        tail_yt(g - 1, YT_AT.index(s))

            def first2():
                for n in range(A_USES):
                    copy_att2(0, 0, 0, n)

            def last2(g, half, par):
                attention(g, half, par, False)
                act.wait_ge(w3_loaded, 32)
                act.wait_ge(att1_full, BH * G)
                for p in range(PAR):
                    cols = slice(2 * P * p, 2 * P * (p + 1))
                    nc.scalar.activation(wi_hi[:, :, cols], wi[:, :, cols], ACT.Copy)
                    nc.scalar.activation(wo_hi[:, 2 * p:2 * p + 2, :], wo[:, 2 * p:2 * p + 2, :], ACT.Copy).then_inc(w_hi, 1)
                tail_yt(g, 0)
                tail_yt(g, 1)

            groups(act, first2, lambda g, half, par: attention(g, half, par, True), last2)

            def root3(g):
                act.wait_ge(var3, g + 1)
                nc.scalar.activation(ln3[:, 1, :], ln3[:, 0, :], ACT.Sqrt).then_inc(std3, 1)

            def copy_x3(g, par):
                act.wait_ge(x3_transposed, g + 1)
                nc.scalar.activation(x_hi[par][:], ps[:, 0:2, :], ACT.Copy).then_inc(x_rounded, 1)

            def silus(g, p):
                for m in range(2):
                    if m == 0:
                        act.wait_ge(dec_ready, PAR * g + p + 1)
                    else:
                        act.wait_ge(logit_full, WT * g + 2 * p + 2)
                    need(act, masked_ready, WT * g + 2 * (p - 2) + m + 1)
                    nc.scalar.activation(acts[p % 2][m][:], ps[:, 2 + m, :], ACT.Silu,
                                         bias=small[:, 8 + 2 * p + m:9 + 2 * p + m]).then_inc(acts_ready, 1)

            def high(g, p):
                for m in range(2):
                    act.wait_ge(masked_ready, WT * g + 2 * p + m + 1)
                    need(act, ffn_full, PAR * g + p - 1)
                    nc.scalar.activation(m_hi[p % 2][m][:], masked[p % 2][m][:], ACT.Copy).then_inc(hi_ready, 1)

            def first3():
                root3(0)
                copy_x3(0, 0)

            def trees(g, half, par, following):
                for p in range(PAR + 1):
                    if p < PAR:
                        silus(g, p)
                    if p >= 1:
                        high(g, p - 1)
                    if p == 3 and following:
                        root3(g + 1)
                    if p == 6 and following:
                        copy_x3(g + 1, 1 - par)

            groups(act, first3, lambda g, half, par: trees(g, half, par, True),
                   lambda g, half, par: trees(g, half, par, False))

        @block.vector
        def _(dve):
            nc.vector.memset(ps[:, 6:8, :], 0.0).then_inc(psum_clear, 1)
            dve.wait_ge(consts, CONSTS)
            nc.vector.tensor_scalar(small[:, 6:8], small[:, 2:4], QK_SCALE, None, ALU.mult).then_inc(kb_ready, 1)

            dve.wait_ge(ek_loaded, 16)
            links = [0]

            def link(ins):
                links[0] += 1
                ins.then_inc(ek_chain, 1)
                dve.wait_ge(ek_chain, links[0])

            link(nc.vector.tensor_copy(ekp[:, 0, :], ek[:, 0, :]))
            link(nc.vector.tensor_tensor(ek[:, 1, :], ek[:, 0, :], ekp[:, 0, :], ALU.subtract))
            link(nc.vector.tensor_copy(ekp[:, 1, :], ek[:, 1, :]))
            nc.vector.tensor_tensor(ekp[:, 2, :], ek[:, 1, :], ekp[:, 1, :], ALU.subtract).then_inc(ek_split, 1)

            def front1(g, half, par):
                dve.wait_ge(gathered[par], 32 * TILES * (half + 1))
                dve.wait_ge(lora_ready, g + 1)
                need(dve, h_stored[par], 16 * half)
                for m in range(2):
                    ins = nc.vector.scalar_tensor_tensor(
                        h_new[par][:, 2 * m:2 * m + 2, :], ps[:, 1 + m, :].rearrange("p (i c) -> p i c", i=2), LORA_SCALE,
                        staged[par][:, 2 * m:2 * m + 2, :], ALU.mult, ALU.add)
                ins.then_inc(h_made, 1)
                dve.wait_ge(h_made, g + 1)
                need(dve, x_transposed, g)
                layer_norm(dve, g, h_new[par], stats, mv, ln, xn, var_ready, std_ready, xn_ready, dve_chain)

            def back1(g, half, par, u0, u1):
                for u in range(u0, u1):
                    dve.wait_ge(qk_copied, 4 * g + u + 1)
                    nc.vector.tensor_tensor(rest[u % 2][:], x32[u % 2][:], parts[u % 2][:, 0, :], ALU.subtract).then_inc(qk_rest, 1)
                    dve.wait_ge(qk_rest, 4 * g + u + 1)
                    nc.vector.tensor_copy(parts[u % 2][:, 1, :], rest[u % 2][:]).then_inc(qk_part2, 1)
                    dve.wait_ge(qk_part2, 4 * g + u + 1)
                    nc.vector.tensor_tensor(parts[u % 2][:, 2, :], rest[u % 2][:], parts[u % 2][:, 1, :], ALU.subtract).then_inc(qk_part3, 1)

            def low_xt(g, par):
                dve.wait_ge(xt_rounded, g + 1)
                nc.vector.tensor_tensor(xt_lo[par][:], ps[:, 3:5, :], xt_hi[par][:].bitcast(F32), ALU.subtract).then_inc(xt_ready, 1)

            def back1_v(g, half, par, m):
                dve.wait_ge(v_full, 2 * g + m + 1)
                nc.vector.tensor_tensor(v_out[par][:, 2 * m:2 * m + 2, :], ps[:, 7, :].rearrange("p (i c) -> p i c", i=2),
                                            vb[:, :].unsqueeze(1).to_broadcast([P, 2, C]), ALU.add).then_inc(v_copied, 1)

            def first1():
                front1(0, 0, 0)
                dve.wait_ge(wa_rounded, 1)
                nc.vector.tensor_tensor(wa_lo[:], wa[:], wa_hi[:].bitcast(F32), ALU.subtract).then_inc(wa_split, 1)
                low_xt(0, 0)
                front1(1, 0, 1)

            def body1(g, half, par):
                if not beyond(g + 1):
                    low_xt(g + 1, 1 - par)
                back1_v(g, half, par, 0)
                back1(g, half, par, 0, 1)
                if not beyond(g + 2):
                    front1(g + 2, half + 1, par)
                back1(g, half, par, 1, 2)
                back1_v(g, half, par, 1)
                back1(g, half, par, 2, 4)
                if not beyond(g + 1):
                    need(dve, v_stored[1 - par], 16 * (half + par))

            dve.wait_ge(w_loaded, 32)
            dve.wait_ge(psum_clear, 1)
            deep_groups(dve, first1, body1)

            def add(g, half, par, x):
                dve.wait_ge(att1_full, BH * g + x + 1)
                if x == 0:
                    dve.wait_ge(att2_copied, A_USES * (g + 1))
                row = att[par][:, x, :]
                nc.vector.tensor_tensor(row, ps[:, 0, 0:SPAN], row, ALU.add).then_inc(scores_ready, 1)

            def maxima(g, half, par, x):
                dve.wait_ge(st_full, BH * g + x + 1)
                nc.vector.tensor_reduce(neg_max[:, x, :], ps[:, 2 + x % 2, 0:SPAN].rearrange("p (n s) -> p n s", n=3),
                                        AX.X, ALU.max, negate=True).then_inc(maxes, 1)
                dve.wait_ge(maxes, BH * g + x + 1)
                nc.vector.tensor_tensor(neg_max[:, x, 1:2], neg_max[:, x, 1:2], neg_max[:, x, 2:3], ALU.min).then_inc(max_ready, 1)

            def copy_pt(g, half, par, x):
                dve.wait_ge(pt_full, BH * g + x + 1)
                nc.vector.tensor_copy(att[par][:, x, :], ps[:, 4 + x % 2, 0:SPAN]).then_inc(pt_copied[1], 1)

            def copy_y2(g, c):
                dve.wait_ge(y2_full, 4 * g + c + 1)
                need(dve, y2_stored, 128 * g)
                nc.vector.tensor_copy(y2s[:, :, c * JC:(c + 1) * JC],
                                      ps[:, 7 if c % 2 == 0 else 1, :].rearrange("p (j x) -> p x j", x=BH)).then_inc(y2_copied, 1)

            def tail_norm(g, par, a):
                if a == 0:
                    flat = sums[par][:].rearrange("p h b j -> p (h b j)")
                    need(dve, h2_ready, g)
                    nc.vector.reciprocal(flat, flat).then_inc(inv_ready, 1)
                    dve.wait_ge(inv_ready, g + 1)
                dve.wait_ge(y_back, 2 * g + a + 1)
                for j in range(2):
                    ins = nc.vector.tensor_tensor(
                        yn[:, 2 * a + j, :].rearrange("p (h d) -> p h d", h=H),
                        ps[:, 7, j * C:(j + 1) * C].rearrange("p (h d) -> p h d", h=H),
                        sums[par][:, :, a, j:j + 1].to_broadcast([P, H, HD]), ALU.mult)
                ins.then_inc(yn_ready, 1)

            def tail_proj(g, a):
                dve.wait_ge(proj_full, 2 * g + a + 1)
                nc.vector.tensor_tensor(yn[:, 2 * a:2 * a + 2, :], ps[:, 7, :].rearrange("p (i c) -> p i c", i=2),
                                        bp[:, :].unsqueeze(1).to_broadcast([P, 2, C]), ALU.add).then_inc(proj_ready, 1)

            def attention(g, half, par):
                for s in range(STEPS):
                    if s < BH:
                        add(g, half, par, s)
                    if not first(g) and s in (4, 8, 12, 16):
                        copy_y2(g - 1, s // 4 - 1)
                    if 0 <= s - 1 < BH:
                        maxima(g, half, par, s - 1)
                    if BH // 2 <= s - 3 < BH:
                        copy_pt(g, half, par, s - 3)
                    if not first(g):
                        if s - 1 in BACK_AT:
                            tail_norm(g - 1, 1 - par, BACK_AT.index(s - 1))
                        if s - 1 in PROJ_AT:
                            tail_proj(g - 1, PROJ_AT.index(s - 1))

            def last2(g, half, par):
                attention(g, half, par)
                for c in range(4):
                    copy_y2(g, c)
                for p in range(PAR):
                    cols = slice(2 * P * p, 2 * P * (p + 1))
                    dve.wait_ge(w_hi, p + 1)
                    nc.vector.tensor_tensor(wi_lo[:, :, cols], wi[:, :, cols], wi_hi[:, :, cols].bitcast(F32), ALU.subtract)
                    nc.vector.tensor_tensor(wo_lo[:, 2 * p:2 * p + 2, :], wo[:, 2 * p:2 * p + 2, :],
                                            wo_hi[:, 2 * p:2 * p + 2, :].bitcast(F32), ALU.subtract).then_inc(w_split, 1)
                for a in range(2):
                    tail_norm(g, par, a)
                for a in range(2):
                    tail_proj(g, a)

            dve.wait_ge(w2_loaded, 48)
            groups(dve, lambda: None, attention, last2)

            dve.wait_ge(tree_loaded, 16)
            nc.vector.tensor_copy(tree[:], treef[:]).then_inc(tree_ready, 1)

            def front3(g, half, par):
                dve.wait_ge(h3_loaded[par], 16 * (half + 1))
                need(dve, x3_transposed, g)
                layer_norm(dve, g, h3[par], stats3, mv3, ln3, xn3, var3, std3, xn3_ready, chain3)

            def decide(g, p):
                dve.wait_ge(logit_full, WT * g + 2 * p + 1)
                need(dve, reach_full, WT * g + 2 * (p - 1))
                b = small[:, 8 + 2 * p:9 + 2 * p]
                nc.vector.tensor_scalar(dec[p % 2][:], ps[:, 2, :], b, 0.0, ALU.add, ALU.is_gt).then_inc(dec_ready, 1)

            def mask(g, p):
                for m in range(2):
                    dve.wait_ge(reach_full, WT * g + 2 * p + m + 1)
                    dve.wait_ge(acts_ready, WT * g + 2 * p + m + 1)
                    need(dve, lo_ready, WT * g + 2 * (p - 2) + m + 1)
                    nc.vector.scalar_tensor_tensor(masked[p % 2][m][:], ps[:, 4 + m, :], small[:, 24 + m:25 + m],
                                                   acts[p % 2][m][:], ALU.is_ge, ALU.mult).then_inc(masked_ready, 1)

            def low(g, p):
                for m in range(2):
                    dve.wait_ge(hi_ready, WT * g + 2 * p + m + 1)
                    need(dve, ffn_full, PAR * g + p - 1)
                    nc.vector.tensor_tensor(m_lo[p % 2][m][:], masked[p % 2][m][:], m_hi[p % 2][m][:].bitcast(F32),
                                            ALU.subtract).then_inc(lo_ready, 1)

            def low_x3(g, par):
                dve.wait_ge(x_rounded, g + 1)
                nc.vector.tensor_tensor(x_lo[par][:], ps[:, 0:2, :], x_hi[par][:].bitcast(F32), ALU.subtract).then_inc(xt3_ready, 1)

            def finish(g, half, par):
                dve.wait_ge(ffn_full, PAR * (g + 1))
                for m in range(2):
                    ins = nc.vector.tensor_tensor(o3[par][:, 2 * m:2 * m + 2, :], ps[:, 6 + m, :].rearrange("p (i c) -> p i c", i=2),
                                                  h3[par][:, 2 * m:2 * m + 2, :], ALU.add)
                ins.then_inc(out_ready, 1)

            def trees(g, half, par, following):
                for p in range(PAR + 2):
                    if p < PAR:
                        decide(g, p)
                    if 1 <= p <= PAR:
                        mask(g, p - 1)
                    if p >= 2:
                        low(g, p - 2)
                    if p == 3 and following:
                        front3(g + 1, half + par, 1 - par)
                    if p == 7 and following:
                        low_x3(g + 1, 1 - par)
                finish(g, half, par)
                if following:
                    need(dve, out_stored[1 - par], 16 * (half + par))

            def first3():
                front3(0, 0, 0)
                low_x3(0, 0)

            groups(dve, first3, lambda g, half, par: trees(g, half, par, True),
                   lambda g, half, par: trees(g, half, par, False))

        @block.tensor
        def _(pe):
            pe.wait_ge(consts, CONSTS)
            pe.wait_ge(w_loaded, 32)

            def front1_a(g, half, par):
                pe.wait_ge(gathered[par], 32 * TILES * (half + 1))
                need(pe, at_copied, g)
                need(pe, lora_ready, g)
                for i in range(TILES):
                    ins = nc.tensor.transpose(ps[0:RANK, 0, i * P:(i + 1) * P], staged_a[par][:, i, :], ident[:])
                ins.then_inc(a_transposed, 1)

            def front1_lora(g):
                pe.wait_ge(at_copied, g + 1)
                need(pe, h_made, g)
                for i in range(TILES):
                    ins = nc.tensor.matmul(ps[:, 1 + i // 2, (i % 2) * C:(i % 2 + 1) * C], at[:, i * P:(i + 1) * P],
                                           lb[:], start=True, stop=True)
                ins.then_inc(lora_ready, 1)

            def front1_x(g, half, par):
                pe.wait_ge(xn_ready, g + 1)
                need(pe, xt_ready, g)
                for m in range(CM):
                    for i in range(TILES):
                        ins = nc.tensor.transpose(ps[:, 3 + m, i * P:(i + 1) * P], xn[:, i, m * P:(m + 1) * P], ident[:])
                ins.then_inc(x_transposed, 1)

            def qk(g, half, par, u0, u1):
                for u in range(u0, u1):
                    need(pe, qk_copied, 4 * g + u - 1)
                    terms = [(a, b, m) for m in range(CM) for a, b in ((wa_hi, xt_hi), (wa_lo, xt_hi), (wa_hi, xt_lo))]
                    for n, (a, b, m) in enumerate(terms):
                        ins = nc.tensor.matmul(ps[:, 5 + u % 2, :], a[:, m, u * P:(u + 1) * P], b[par][:, m, :],
                                               start=(n == 0), stop=(n == len(terms) - 1))
                    ins.then_inc(qk_full, 1)

            def value(g, half, par, a):
                need(pe, v_copied, 2 * g + a)
                terms = [(x, w, m) for m in range(CM) for x, w in ((xt_hi, wa_hi), (xt_hi, wa_lo), (xt_lo, wa_hi))]
                for i in range(2):
                    t = 2 * a + i
                    for n, (x, w, m) in enumerate(terms):
                        ins = nc.tensor.matmul(ps[:, 7, i * C:(i + 1) * C], x[par][:, m, t * P:(t + 1) * P],
                                               w[:, m, 2 * C:3 * C], start=(n == 0), stop=(n == len(terms) - 1))
                ins.then_inc(v_full, 1)

            def first1():
                front1_a(0, 0, 0)
                front1_lora(0)
                front1_a(1, 0, 1)
                front1_x(0, 0, 0)
                front1_lora(1)
                pe.wait_ge(wa_split, 1)

            def body1(g, half, par):
                if not beyond(g + 1):
                    front1_x(g + 1, half + par, 1 - par)
                if not beyond(g + 2):
                    front1_a(g + 2, half + 1, par)
                pe.wait_ge(xt_ready, g + 1)
                value(g, half, par, 0)
                qk(g, half, par, 0, 1)
                if not beyond(g + 2):
                    front1_lora(g + 2)
                qk(g, half, par, 1, 2)
                value(g, half, par, 1)
                qk(g, half, par, 2, 4)

            pe.wait_ge(psum_clear, 1)
            deep_groups(pe, first1, body1)

            def relative_keys(g, half, par, n):
                if n == 0:
                    pe.wait_ge(q_loaded[par], 16 * len(Q_PARTS) * (half + 1))
                need(pe, att2_copied, A_USES * g + n)
                if n == 0:
                    need(pe, y2_copied, 4 * (g - 1))
                for j in range(JC):
                    col = n * JC + j
                    u = col if col < T else col - T
                    t = col if col < T else col - P
                    ins = nc.tensor.matmul(ps[:, 1, j * BH:(j + 1) * BH], r_stack[:, T - 1 - u:T - 1 - u + P],
                                           q_stack[par][:, :, t], start=True, stop=True)
                ins.then_inc(att2_full, 1)

            def keys(g, half, par, x):
                if x % (BH // 2) == 0:
                    pe.wait_ge(k_loaded[x // (BH // 2)], 16 * len(K_PARTS) * (g + 1))
                need(pe, scores_ready, BH * g + x)
                nc.tensor.matmul(ps[:, 0, 0:T], k_stack[:, x, 0:P], q_stack[par][0:KS, x, :], start=True, stop=True)
                nc.tensor.matmul(ps[:, 0, T:SPAN], k_stack[:, x, P:T], q_stack[par][0:KS, x, P:T],
                                 start=True, stop=True).then_inc(att1_full, 1)

            def copied(g, x):
                return pt_copied[x // (BH // 2)], BH // 2 * g + x % (BH // 2) + 1

            def to_rows(g, half, par, x):
                pe.wait_ge(scores_ready, BH * g + x + 1)
                need(pe, exp_done, BH * g + x - 1)
                for n in range(3):
                    ins = nc.tensor.transpose(ps[:, 2 + x % 2, n * P:(n + 1) * P], att[par][:, x, n * P:(n + 1) * P], ident[:])
                ins.then_inc(st_full, 1)

            def to_columns(g, half, par, x):
                pe.wait_ge(exp_done, BH * g + x + 1)
                if x >= 2:
                    pe.wait_ge(*copied(g, x - 2))
                else:
                    need(pe, pt_copied[1], BH // 2 * g)
                for n in range(3):
                    ins = nc.tensor.transpose(ps[:, 4 + x % 2, n * P:(n + 1) * P], probs[x % 2][:, n * P:(n + 1) * P], ident[:])
                ins.then_inc(pt_full, 1)

            def values(g, half, par, x):
                h, b = x // GB, x % GB
                q = h % 4
                if x == 0:
                    pe.wait_ge(v_loaded[par], 16 * (half + 1))
                if x % BLOCK == 0:
                    need(pe, y1_copied, 4 * g + x // BLOCK)
                pe.wait_ge(*copied(g, x))
                vh = v_in[par]
                nc.tensor.matmul(ps[32 * q:32 * q + HD, 6, b * T:(b + 1) * T], vh[:, 2 * b, h * HD:(h + 1) * HD],
                                 att[par][:, x, 0:T], start=(b == 0), stop=False, skip_group_check=True)
                ins = nc.tensor.matmul(ps[32 * q:32 * q + HD, 6, b * T + P:(b + 1) * T], vh[:, 2 * b + 1, h * HD:(h + 1) * HD],
                                       att[par][:, x, T:SPAN], start=False, stop=True, skip_group_check=True)
                if x % BLOCK == BLOCK - 1:
                    ins.then_inc(y1_full, 1)

            def relative_values(g, par, c, j0, j1):
                if j0 == 0:
                    if c == 0:
                        need(pe, proj_ready, 2 * g)
                    elif c == 1:
                        pe.wait_ge(att2_copied, A_USES * (g + 1 if last(g) else g + 2))
                    else:
                        pe.wait_ge(y2_copied, 4 * g + c - 1)
                for j in range(j0, j1):
                    for q in range(4):
                        t = q * QT + c * JC + j
                        o = ps[32 * q:32 * q + HD, 7 if c % 2 == 0 else 1, j * BH:(j + 1) * BH]
                        ins = nc.tensor.matmul(o, rv[:, T - 1 - t, :], att[par][:, :, t], start=(j == 0), stop=(t < P),
                                               skip_group_check=True)
                        if t >= P:
                            ins = nc.tensor.matmul(o, rv[:, T - 1 - (t - P), :], att[par][:, :, t + P], start=False, stop=True,
                                                   skip_group_check=True)
                if j1 == JC:
                    ins.then_inc(y2_full, 1)

            def tail_back(g, a):
                if a == 0:
                    pe.wait_ge(y_summed, g + 1)
                    pe.wait_ge(y2_copied, 4 * (g + 1))
                else:
                    pe.wait_ge(yn_ready, 2 * g + 1)
                for j in range(2):
                    for m in range(CM):
                        t = 2 * a + j
                        ins = nc.tensor.transpose(ps[:, 7, j * C + m * P:j * C + (m + 1) * P], y1c[:, m, t * P:(t + 1) * P], ident[:])
                ins.then_inc(y_back, 1)

            def tail_yt(g, m):
                if m == 0:
                    pe.wait_ge(yn_ready, 2 * (g + 1))
                else:
                    pe.wait_ge(yt_copied, 2 * g + 1)
                for i in range(TILES):
                    ins = nc.tensor.transpose(ps[:, 7, i * P:(i + 1) * P], yn[:, i, m * P:(m + 1) * P], ident[:])
                ins.then_inc(yt_full, 1)

            def tail_proj(g, a):
                if a == 0:
                    pe.wait_ge(yt_copied, 2 * (g + 1))
                else:
                    pe.wait_ge(proj_ready, 2 * g + 1)
                for i in range(2):
                    for m in range(CM):
                        t = 2 * a + i
                        ins = nc.tensor.matmul(ps[:, 7, i * C:(i + 1) * C], yt[:, m, t * P:(t + 1) * P], wp[:, m, :],
                                               start=(m == 0), stop=(m == CM - 1))
                ins.then_inc(proj_full, 1)

            def attention(g, half, par, following):
                for s in range(STEPS):
                    more = A_AT.get(s, ()) if following else ()
                    if s < BH:
                        keys(g, half, par, s)
                    if 0 <= s - 1 < BH:
                        to_rows(g, half, par, s - 1)
                    for n in more[:1]:
                        relative_keys(g + 1, half + par, 1 - par, n)
                    if 0 <= s - 3 < BH:
                        to_columns(g, half, par, s - 3)
                    if not first(g) and s < 16:
                        relative_values(g - 1, 1 - par, s // 4, s % 4 * 4, s % 4 * 4 + 4)
                    if 0 <= s - 5 < BH:
                        values(g, half, par, s - 5)
                    for n in more[1:]:
                        relative_keys(g + 1, half + par, 1 - par, n)
                    if not first(g):
                        for step, at_steps in ((tail_back, BACK_AT), (tail_yt, YT_PE_AT), (tail_proj, PROJ_AT)):
                            if s in at_steps:
                                step(g - 1, at_steps.index(s))

            def first2():
                for n in range(A_USES):
                    relative_keys(0, 0, 0, n)

            def last2(g, half, par):
                attention(g, half, par, False)
                for c in range(4):
                    relative_values(g, par, c, 0, JC)
                for step in (tail_back, tail_yt, tail_proj):
                    step(g, 0)
                    step(g, 1)

            pe.wait_ge(w2_loaded, 48)
            pe.wait_ge(ones_ready, 5)
            pe.wait_ge(ek_stacked, 16 * len(K_PARTS))
            groups(pe, first2, lambda g, half, par: attention(g, half, par, True), last2)

            def front3(g, half, par):
                pe.wait_ge(xn3_ready, g + 1)
                need(pe, xt3_ready, g)
                for m in range(CM):
                    for i in range(TILES):
                        ins = nc.tensor.transpose(ps[:, m, i * P:(i + 1) * P], xn3[:, i, m * P:(m + 1) * P], ident[:])
                ins.then_inc(x3_transposed, 1)

            def logits(g, par, p):
                for m in range(2):
                    need(pe, acts_ready, WT * g + 2 * (p - 1) + m + 1)
                    if m == 0:
                        need(pe, dec_ready, PAR * g + p)
                    if first(g) and m == 0:
                        pe.wait_ge(w_split, p + 1)
                    w = (2 * p + m) * P
                    terms = [(a, b, k) for k in range(CM) for a, b in ((wi_hi, x_hi), (wi_lo, x_hi), (wi_hi, x_lo))]
                    for n, (a, b, k) in enumerate(terms):
                        ins = nc.tensor.matmul(ps[:, 2 + m, :], a[:, k, w:w + P], b[par][:, k, :], start=(n == 0),
                                               stop=(n == len(terms) - 1))
                    ins.then_inc(logit_full, 1)

            def reach(g, p):
                pe.wait_ge(dec_ready, PAR * g + p + 1)
                for m in range(2):
                    need(pe, masked_ready, WT * g + 2 * (p - 1) + m + 1)
                    nc.tensor.matmul(ps[:, 4 + m, :], tree[:, m * P:(m + 1) * P], dec[p % 2][:], start=True, stop=True).then_inc(reach_full, 1)

            def combine(g, p):
                for m in range(2):
                    pe.wait_ge(lo_ready, WT * g + 2 * p + m + 1)
                    if p == 0 and m == 0:
                        need(pe, out_ready, g)
                    for i in range(TILES):
                        for n, (a, b) in enumerate(((m_hi, wo_hi), (m_hi, wo_lo), (m_lo, wo_hi))):
                            ins = nc.tensor.matmul(
                                ps[:, 6 + i // 2, (i % 2) * C:(i % 2 + 1) * C], a[p % 2][m][:, i * P:(i + 1) * P],
                                b[:, 2 * p + m, :], start=(p == 0 and m == 0 and i % 2 == 0 and n == 0),
                                stop=(p == PAR - 1 and m == 1 and n == 2), skip_group_check=True)
                ins.then_inc(ffn_full, 1)

            def trees(g, half, par, following):
                pe.wait_ge(xt3_ready, g + 1)
                for p in range(PAR + 3):
                    if p < PAR:
                        logits(g, par, p)
                    if 1 <= p <= PAR:
                        reach(g, p - 1)
                    if p >= 3:
                        combine(g, p - 3)
                    if p == 6 and following:
                        front3(g + 1, half, 1 - par)

            pe.wait_ge(tree_ready, 1)
            groups(pe, lambda: front3(0, 0, 0), lambda g, half, par: trees(g, half, par, True),
                   lambda g, half, par: trees(g, half, par, False))


def tree_constants():
    tree, turns = np.zeros((P, 2 * P), np.float32), np.zeros((2 * P,), np.float32)
    for n in range(2 ** (DEPTH + 1) - 1):
        col = n if n < P - 1 else n + 1
        at = n
        while at:
            up, right = (at - 1) // 2, at % 2 == 0
            tree[up, col] = 1.0 if right else -1.0
            turns[col] += right
            at = up
    return tree, np.ascontiguousarray((turns - 0.5).reshape(2, P).T)


def kernel(x, L0_tok_weight, L0_tok_lora_A, L0_tok_lora_B, L0_attn_Wattn, L0_attn_battn, L0_attn_Wproj,
           L0_attn_bproj, L0_attn_embk, L0_attn_embv, L0_ffn_W_in, L0_ffn_b_in, L0_ffn_W_out):
    import concourse.bacc as bacc
    from concourse.bass_utils import run_bass_kernel_spmd

    def by_tile(a):
        a = a.reshape(PAR, 2 * P - 1, -1)
        gap = np.zeros((PAR, 1, a.shape[2]), a.dtype)
        return np.concatenate([a[:, :P - 1], gap, a[:, P - 1:]], axis=1).reshape(WT * P, -1)

    x = np.asarray(x)
    tree, thresholds = tree_constants()
    embv = np.asarray(L0_attn_embv)
    arrays = {
        "idx": x.reshape(TOK // P, P).T,
        "tok_w": L0_tok_weight,
        "lora_a": L0_tok_lora_A,
        "lora_b": L0_tok_lora_B,
        "wattn": L0_attn_Wattn,
        "battn": np.asarray(L0_attn_battn).reshape(6, P).T,
        "vbias": np.asarray(L0_attn_battn)[2 * C:].reshape(1, C),
        "wproj": L0_attn_Wproj,
        "bproj": np.asarray(L0_attn_bproj).reshape(1, C),
        "embk_rev": np.asarray(L0_attn_embk)[::-1].T,
        "embv_pad": np.concatenate([embv[::-1], np.zeros((P - 1, HD), embv.dtype)]),
        "w_in": by_tile(np.asarray(L0_ffn_W_in)).T,
        "b_in": by_tile(np.asarray(L0_ffn_b_in)).reshape(WT, P).T,
        "w_out": by_tile(np.asarray(L0_ffn_W_out).T),
        "ident_in": np.eye(P, dtype=np.float32),
        "tree_in": tree,
        "thr_in": thresholds,
    }
    arrays = {k: np.ascontiguousarray(v) for k, v in arrays.items()}
    nc = bacc.Bacc("TRN2", target_bir_lowering=False, num_devices=1)
    args = [nc.dram_tensor(k, v.shape, mybir.dt.from_np(v.dtype), kind="ExternalInput").ap() for k, v in arrays.items()]
    out = nc.dram_tensor("out", (TOK, C), F32, kind="ExternalOutput").ap()
    tower_kernel(nc, *args, out)
    r = run_bass_kernel_spmd(nc, [arrays], core_ids=[0])
    return r.results[0]["out"].reshape(BATCH, T, C)
```

```python
import math
import numpy as np
import concourse.bass as bass
from concourse import mybir
from contextlib import ExitStack

F32 = mybir.dt.float32
BF16 = mybir.dt.bfloat16
F32R = mybir.dt.float32r
U32 = mybir.dt.uint32
ALU = mybir.AluOpType
ACT = mybir.ActivationFunctionType
AX = mybir.AxisListType

P = 128
BATCH, T, C, H = 16, 256, 256, 16
HD = C // H
TOK = BATCH * T
G = 8
GT = TOK // G
TILES = GT // P
GB = GT // T
BH = GB * H
CM = C // P
RANK = 8
LORA_SCALE = 8 / math.sqrt(RANK)
QK_SCALE = 1 / math.sqrt(HD)
EPS = 1e-5
PAR, DEPTH = 8, 7
WT = 2 * PAR
Q_PARTS = (0, 0, 1, 1, 0, 2)
K_PARTS = (0, 1, 0, 1, 2, 0)
KS = len(Q_PARTS) * HD
MASK = -1e30
SPAN = T + P
BLOCK = 8
JC = 16
QT = T // 4


def need(eng, sem, count):
    if not (isinstance(count, int) and count <= 0):
        eng.wait_ge(sem, count)


def apart(eng, waits_done):
    eng.sem_inc(waits_done, 1)


def deep_groups(eng, prologue, body):
    prologue()
    body(0, 0, 0)
    body(1, 0, 1)
    with eng.Fori(0, 2) as i:
        body(i * 2 + 2, i + 1, 0)
        body(i * 2 + 3, i + 1, 1)
    body(6, 3, 0)
    body(7, 3, 1)


def beyond(g):
    return isinstance(g, int) and g >= G


def last(g):
    return isinstance(g, int) and g == G - 1


def first(g):
    return isinstance(g, int) and g == 0


def groups(eng, prologue, body, epilogue):
    prologue()
    body(0, 0, 0)
    with eng.Fori(0, 3) as i:
        body(i * 2 + 1, i, 1)
        body(i * 2 + 2, i + 1, 0)
    epilogue(G - 1, G // 2 - 1, 1)


def tower_kernel(nc, idx, tok_w, lora_a, lora_b, wattn, battn, vbias, wproj, bproj, embk_rev, embv_pad,
                 w_in, b_in, w_out, ident_in, tree_in, thr_in, out):
    ctx = ExitStack()
    with ctx:
        def sb(name, shape, dt=F32):
            return ctx.enter_context(nc.sbuf_tensor(name, shape, dt))

        def sem(name):
            return ctx.enter_context(nc.semaphore(name))

        def two(name):
            return [sem(f"{name}{n}") for n in range(2)]

        h_d = nc.dram_tensor("h_d", (TOK, C), F32, kind="Internal").ap()
        h2_d = nc.dram_tensor("h2_d", (TOK, C), F32, kind="Internal").ap()
        v_d = nc.dram_tensor("v_d", (TOK, C), F32, kind="Internal").ap()
        qk_d = nc.dram_tensor("qk_d", (2, 3, C, TOK), BF16, kind="Internal").ap()
        y1_d = nc.dram_tensor("y1_d", (C, TOK), F32, kind="Internal").ap()
        y2_d = nc.dram_tensor("y2_d", (C, TOK), F32, kind="Internal").ap()

        ps = ctx.enter_context(nc.psum_tensor("ps", [P, 8, 512], F32))

        def rows(dram, g):
            return dram[bass.ds(g * GT, GT), :].rearrange("(i p) c -> p i c", p=P)

        ident = sb("ident", [P, P])
        small = sb("small", [P, 32])
        consts = sem("consts")
        kb_ready = sem("kb_ready")
        psum_clear = sem("psum_clear")
        CONSTS = 16 * 5

        sp_waited, pool_waited, dve_waited = sem("sp_waited"), sem("pool_waited"), sem("dve_waited")

        idx_sb = sb("idx_sb", [P, TOK // P], mybir.dt.int32)
        idx_g = [sb(f"idx_g{n}", [P, TILES], mybir.dt.int32) for n in range(2)]
        idx_loaded, idx_ready = sem("idx_loaded"), sem("idx_ready")

        stage1 = ExitStack()

        def sb1(name, shape, dt=F32):
            return stage1.enter_context(nc.sbuf_tensor(name, shape, dt))

        w_loaded = sem("w_loaded")
        gathered, gathered_a = two("gathered"), two("gathered_a")
        a_transposed, at_copied, lora_ready, h_made = (sem(n) for n in ("a_transposed", "at_copied", "lora_ready", "h_made"))
        var_ready, std_ready, xn_ready, x_transposed, xt_ready = (sem(n) for n in ("var_ready", "std_ready", "xn_ready", "x_transposed", "xt_ready"))
        qk_full, qk_copied, qk_rest, qk_part2, qk_part3 = (sem(n) for n in ("qk_full", "qk_copied", "qk_rest", "qk_part2", "qk_part3"))
        v_full, v_copied, wa_rounded, wa_split, xt_rounded = (sem(n) for n in ("v_full", "v_copied", "wa_rounded", "wa_split", "xt_rounded"))
        h_stored, v_stored, parts_stored = two("h_stored"), two("v_stored"), [sem(f"parts_stored{n}") for n in range(4)]
        dve_chain, ek_chain = sem("dve_chain"), sem("ek_chain")

        wa = sb1("wa", [P, CM, 3 * C])
        vb = sb1("vb", [P, C])
        lb = sb1("lb", [RANK, C])
        staged = [sb1(f"staged{n}", [P, TILES, C]) for n in range(2)]
        staged_a = [sb1(f"staged_a{n}", [P, TILES, RANK]) for n in range(2)]
        at = sb1("at", [RANK, GT])
        h_new = [sb1(f"h_new{n}", [P, TILES, C]) for n in range(2)]
        stats = sb1("stats", [P, TILES, 6])
        mv = sb1("mv", [P, TILES, 2])
        ln = sb1("ln", [P, 4, TILES])
        xn = sb1("xn", [P, TILES, C])
        wa_hi, wa_lo = sb1("wa_hi", [P, CM, 3 * C], F32R), sb1("wa_lo", [P, CM, 3 * C], F32R)
        xt_hi = [sb1(f"xt_hi{n}", [P, CM, GT], F32R) for n in range(2)]
        xt_lo = [sb1(f"xt_lo{n}", [P, CM, GT], F32R) for n in range(2)]
        x32 = [sb1(f"x32_{n}", [P, GT]) for n in range(4)]
        rest = [sb1(f"rest{n}", [P, GT]) for n in range(2)]
        parts = [sb1(f"parts{n}", [P, 3, GT], BF16) for n in range(4)]
        v_out = [sb1(f"v_out{n}", [P, TILES, C]) for n in range(2)]
        stage1_stored = [(h_stored, 16 * G // 2), (v_stored, 16 * G // 2), (parts_stored, 16 * G)]
        LN_LINKS = 7

        def layer_norm(dve, call, src, st, mvt, lnt, dst, variance, std, done, chain, between=lambda: None):
            n = [call * LN_LINKS]

            def link(ins):
                n[0] = n[0] + 1
                ins.then_inc(chain, 1)
                dve.wait_ge(chain, n[0])

            for i in range(TILES):
                ins = nc.vector.bn_stats(st[:, i, :], src[:, i, :])
            link(ins)
            apart(dve, dve_waited)
            for i in range(TILES):
                ins = nc.vector.bn_aggr(mvt[:, i, :], st[:, i, :])
            link(ins)
            nc.vector.tensor_scalar(lnt[:, 0, :], mvt[:, :, 1], EPS, None, ALU.add).then_inc(variance, 1)
            between()
            dve.wait_ge(std, call + 1)
            link(nc.vector.reciprocal(lnt[:, 2, :], lnt[:, 1, :]))
            link(nc.vector.tensor_tensor(lnt[:, 3, :], lnt[:, 2, :], lnt[:, 2, :], ALU.mult))
            link(nc.vector.tensor_tensor(lnt[:, 3, :], lnt[:, 3, :], lnt[:, 0, :], ALU.mult))
            link(nc.vector.tensor_scalar(lnt[:, 3, :], lnt[:, 3, :], -0.5, 1.5, ALU.mult, ALU.add))
            link(nc.vector.tensor_tensor(lnt[:, 2, :], lnt[:, 2, :], lnt[:, 3, :], ALU.mult))
            for i in range(TILES):
                ins = nc.vector.tensor_scalar(dst[:, i, :], src[:, i, :], mvt[:, i, 0:1], lnt[:, 2, i:i + 1],
                                              ALU.subtract, ALU.mult)
            link_last = ins
            link_last.then_inc(done, 1)

        stage1.close()
        stage2 = ExitStack()

        def sb2(name, shape, dt=F32):
            return stage2.enter_context(nc.sbuf_tensor(name, shape, dt))

        stage1_done = sem("stage1_done")
        att = [sb2(f"att{n}", [P, BH, SPAN]) for n in range(2)]
        q_stack = [sb2(f"q_stack{n}", [KS + 1, BH, T], BF16) for n in range(2)]
        k_stack = sb2("k_stack", [KS, BH, T], BF16)
        r_stack = sb2("r_stack", [KS + 1, SPAN], BF16)
        ekp = sb2("ekp", [HD, 3, T], BF16)
        rv = sb2("rv", [P, T, HD])
        wp = sb2("wp", [P, CM, C])
        bp = sb2("bp", [P, C])
        v_in = [sb2(f"v_in{n}", [P, TILES, C]) for n in range(2)]
        neg_max = sb2("neg_max", [P, BH, 3])
        sums = [sb2(f"sums{n}", [P, H, GB, 2]) for n in range(2)]
        probs = [sb2(f"probs{n}", [P, SPAN]) for n in range(2)]
        y1s = sb2("y1s", [P, H // 4, GT])
        y2s = sb2("y2s", [P, BH, QT])
        ek = y1s[0:HD, 0, :].rearrange("d (n t) -> d n t", n=2)
        y1c = sb2("y1c", [P, CM, GT])
        y2c = sb2("y2c", [P, CM, GT])
        yn = sb2("yn", [P, TILES, C])
        yt = y2c
        hin = y1c[:, :, :].rearrange("p m t -> p (m t)").rearrange("p (i c) -> p i c", i=TILES)

        w2_loaded, ek_loaded, ek_split, ek_stacked = sem("w2_loaded"), sem("ek_loaded"), sem("ek_split"), sem("ek_stacked")
        ones_ready = sem("ones_ready")
        q_loaded, v_loaded = two("q_loaded"), two("v_loaded")
        k_loaded, h_loaded = two("k_loaded"), sem("h_loaded")
        att2_by_dve = sem("att2_by_dve")
        att2_full, att2_copied, att1_full, scores_ready = (sem(n) for n in ("att2_full", "att2_copied", "att1_full", "scores_ready"))
        st_full, maxes, max_ready, exp_done, pt_full = (sem(n) for n in ("st_full", "maxes", "max_ready", "exp_done", "pt_full"))
        pt_copied = two("pt_copied")
        y1_full, y1_copied, y1_stored, y2_full, y2_copied, y2_stored = (sem(n) for n in ("y1_full", "y1_copied", "y1_stored", "y2_full", "y2_copied", "y2_stored"))
        yc_loaded, y_summed, inv_ready = sem("yc_loaded"), sem("y_summed"), sem("inv_ready")
        y_back, yn_ready, yt_full, yt_copied, proj_full, proj_ready, h2_ready, h2_stored = (
            sem(n) for n in ("y_back", "yn_ready", "yt_full", "yt_copied", "proj_full", "proj_ready", "h2_ready", "h2_stored"))
        A_USES = SPAN // JC
        ROUND_AT = 29
        Y2_ENDS = (0, 6, 11, 16, 22, 27, 32, 37, 42, 48, 53, 58, 64)
        Y2_AT = {3 + k: Y2_ENDS[k:k + 2] for k in range(len(Y2_ENDS) - 1)}
        Y2_COPY_AT = (6, 9, 12, 15)
        A_ORDER = [n for c in range(4) for n in range(c, A_USES, 4)]
        A_AT = {6 + k: k for k in range(A_USES)}
        BACK_AT, YT_AT, PROJ_AT = (22, 23), (25, 26), (27, 28, 29, 30)
        COPIES = [0 if x < 4 or x >= BH - 3 or x in (13, 16, 20, 27) else 1 for x in range(BH)]

        def copied(g, x):
            if x < 0:
                return copied(g - 1, x + BH)
            e = COPIES[x]
            return pt_copied[e], COPIES.count(e) * g + COPIES[:x + 1].count(e)

        def a_bank(g, k):
            return k % 4 if first(g) else 1

        def att2_copies(g):
            return A_USES * g - A_USES // 2 if not first(g) else 0

        def y2_bank(g, c):
            return 1 if last(g) and c % 2 == 1 else 7

        def tail_bank(g):
            return 0 if last(g) else 7

        def lagged(g, par, s, lag):
            if s >= lag:
                return [] if beyond(g) else [(g, par, s - lag)]
            return [] if first(g) else [(g - 1, 1 - par, s - lag + BH)]

        stage2.close()
        stage3 = ExitStack()

        def sb3(name, shape, dt=F32):
            return stage3.enter_context(nc.sbuf_tensor(name, shape, dt))

        wo_hi = sb3("wo_hi", [P, WT, C], F32R)
        raw = ExitStack()
        wi = raw.enter_context(nc.sbuf_tensor("wi", [P, CM, WT * P], F32))
        wo = raw.enter_context(nc.sbuf_tensor("wo", [P, WT, C], F32))
        raw.close()
        treef = sb3("treef", [P, 2 * P])
        tree = sb3("tree", [P, 2 * P], BF16)
        xn3 = sb3("xn3", [P, TILES, C])
        x_hi, x_lo = [sb3("x_hi0", [P, CM, GT], F32R)], [sb3("x_lo0", [P, CM, GT], F32R)]
        acts = [[sb3(f"acts{n}{m}", [P, GT]) for m in range(2)] for n in range(2)]
        dec = [sb3(f"dec{n}", [P, GT], BF16) for n in range(2)]
        used = 4 * (WT * C + 2 * P + TILES * C + 2 * CM * GT + 4 * GT) + 2 * (2 * P + 2 * GT)
        sb3("gap_att0", [P, BH * SPAN - used // 4])
        x_hi.append(sb3("x_hi1", [P, CM, GT], F32R))
        x_lo.append(sb3("x_lo1", [P, CM, GT], F32R))
        o3 = [sb3(f"o3_{n}", [P, TILES, C]) for n in range(2)]
        masked = [[sb3(f"masked{n}{m}", [P, GT]) for m in range(2)] for n in range(2)]
        m_hi = [[sb3(f"m_hi{n}{m}", [P, GT], F32R) for m in range(2)] for n in range(2)]
        m_lo = [[sb3(f"m_lo{n}{m}", [P, GT], F32R) for m in range(2)] for n in range(2)]
        sb3("gap_att1", [P, BH * SPAN - 2 * CM * GT - 2 * TILES * C - 12 * GT])
        wi_hi = sb3("wi_hi", [P, CM, WT * P], F32R)
        wi_lo = sb3("wi_lo", [P, CM, WT * P], F32R)
        wo_lo = sb3("wo_lo", [P, WT, C], F32R)
        stats3 = sb3("stats3", [P, TILES, 6])
        mv3 = sb3("mv3", [P, TILES, 2])
        ln3 = sb3("ln3", [P, 4, TILES])
        h3 = v_in
        stage3.close()
        w3_loaded, tree_loaded, tree_ready, w_hi, w_split = (sem(n) for n in ("w3_loaded", "tree_loaded", "tree_ready", "w_hi", "w_split"))
        x_rounded, hi_ready, lo_ready = (sem(n) for n in ("x_rounded", "hi_ready", "lo_ready"))
        h3_loaded, out_stored = two("h3_loaded"), two("out_stored")
        var3, std3, xn3_ready, x3_transposed, xt3_ready = (sem(n) for n in ("var3", "std3", "xn3_ready", "x3_transposed", "xt3_ready"))
        logit_full, dec_ready, acts_ready, reach_full, masked_ready, ffn_full, out_ready = (
            sem(n) for n in ("logit_full", "dec_ready", "acts_ready", "reach_full", "masked_ready", "ffn_full", "out_ready"))
        chain3 = sem("chain3")
        TAIL_BACK_AT, TAIL_YT_AT, TAIL_PROJ_AT = (2, 3), (4, 5), (6, 6, 7, 7)

        block = ctx.enter_context(nc.Block())

        def start_q(eng, g, par):
            for n, p in enumerate(Q_PARTS):
                src = qk_d[0, p, :, bass.ds(g * GT, GT)].rearrange("(h d) t -> d h t", d=HD)
                dst = q_stack[par][n * HD:(n + 1) * HD, :, :]
                eng.dma_start(dst.rearrange("d (h b) t -> d h (b t)", h=H), src).then_inc(q_loaded[par], 16)

        def start_v(eng, g, par):
            eng.dma_start(v_in[par][:], rows(v_d, g)).then_inc(v_loaded[par], 16)

        def start_k(eng, g, part):
            for n, p in enumerate(K_PARTS):
                src = qk_d[1, p, part * C // 2:(part + 1) * C // 2, bass.ds(g * GT, GT)].rearrange("(h d) t -> d h t", d=HD)
                dst = k_stack[n * HD:(n + 1) * HD, part * BH // 2:(part + 1) * BH // 2, :]
                eng.dma_start(dst.rearrange("d (h b) t -> d h (b t)", h=H // 2), src).then_inc(k_loaded[part], 16)

        @block.sync
        def _(sp):
            sp.dma_start(idx_sb[:], idx).then_inc(idx_loaded, 16)
            sp.dma_start(ident[:], ident_in).then_inc(consts, 16)
            sp.dma_start(small[:, 0:6], battn).then_inc(consts, 16)
            sp.dma_start(small[:, 8:8 + WT], b_in).then_inc(consts, 16)
            sp.dma_start(small[:, 24:26], thr_in).then_inc(consts, 16)
            sp.dma_start(lb[:], lora_b).then_inc(consts, 16)
            sp.dma_start(wa[:], wattn.rearrange("(m p) n -> p m n", p=P)).then_inc(w_loaded, 16)
            sp.dma_start(vb[:], vbias.to_broadcast([P, C])).then_inc(w_loaded, 16)

            def store_h(g, half, par):
                sp.wait_ge(h_made, g + 1)
                apart(sp, sp_waited)
                sp.dma_start(rows(h_d, g), h_new[par][:]).then_inc(h_stored[par], 16)

            def store_qkv(g, half, par):
                for u in range(4):
                    sp.wait_ge(qk_part3, 4 * g + u + 1)
                    apart(sp, sp_waited)
                    dst = qk_d[u // 2, :, (u % 2) * P:(u % 2 + 1) * P, bass.ds(g * GT, GT)]
                    sp.dma_start(dst.rearrange("n p t -> p n t"), parts[u][:]).then_inc(parts_stored[u], 16)
                sp.wait_ge(v_copied, 2 * (g + 1))
                apart(sp, sp_waited)
                sp.dma_start(rows(v_d, g), v_out[par][:]).then_inc(v_stored[par], 16)

            def body1(g, half, par):
                if not beyond(g + 2):
                    store_h(g + 2, half + 1, par)
                if last(g):
                    for s in parts_stored:
                        sp.wait_ge(s, 16)
                    sp.wait_ge(v_stored[0], 16)
                    start_q(sp, 0, 0)
                    start_v(sp, 0, 0)
                    start_k(sp, 0, 0)
                    start_k(sp, 0, 1)
                store_qkv(g, half, par)

            def load_q(g, par):
                sp.wait_ge(att1_full, BH * (g - 1))
                apart(sp, sp_waited)
                start_q(sp, g, par)
                need(sp, y1_full, 4 * (g - 1))
                apart(sp, sp_waited)
                start_v(sp, g, par)

            def load_k(g, part):
                sp.wait_ge(att1_full, BH * (g - 1) + BH // 2 * (part + 1))
                apart(sp, sp_waited)
                start_k(sp, g, part)

            def first1():
                store_h(0, 0, 0)
                store_h(1, 0, 1)

            sp.dma_start(ek[:, 0, :], embk_rev).then_inc(ek_loaded, 16)
            sp.dma_start(rv[:], bass.AP(embv_pad.tensor, 0, [[HD, P], [HD, T], [1, HD]])).then_inc(w2_loaded, 16)
            sp.dma_start(wp[:], wproj.rearrange("(m p) n -> p m n", p=P)).then_inc(w2_loaded, 16)
            sp.dma_start(bp[:], bproj.to_broadcast([P, C])).then_inc(w2_loaded, 16)
            deep_groups(sp, first1, body1)
            for pair, count in stage1_stored:
                for s in pair:
                    sp.wait_ge(s, count)
            sp.sem_inc(stage1_done, 1)

            def store_y(g):
                sp.wait_ge(y1_copied, 4 * (g + 1))
                apart(sp, sp_waited)
                for q in range(4):
                    dst = y1_d.rearrange("(a q d) t -> q d a t", q=4, d=HD)[q][:, :, bass.ds(g * GT, GT)]
                    sp.dma_start(dst, y1s[32 * q:32 * q + HD, :, :]).then_inc(y1_stored, 16)
                sp.wait_ge(y2_copied, 4 * (g + 1))
                apart(sp, sp_waited)
                for q in range(4):
                    for b in range(GB):
                        dst = y2_d.rearrange("(h d) t -> d h t", d=HD)[:, :, bass.ds(g * GT + b * T + q * QT, QT)]
                        src = y2s[32 * q:32 * q + HD, :, :].rearrange("p (h b) t -> p b h t", b=GB)[:, b]
                        sp.dma_start(dst, src).then_inc(y2_stored, 16)
                sp.wait_ge(y1_stored, 64 * (g + 1))
                apart(sp, sp_waited)
                need(sp, h2_stored, 16 * g)
                apart(sp, sp_waited)
                sp.dma_start(y1c[:], y1_d[:, bass.ds(g * GT, GT)].rearrange("(m p) t -> p m t", p=P)).then_inc(yc_loaded, 16)
                sp.wait_ge(y2_stored, 128 * (g + 1))
                apart(sp, sp_waited)
                sp.dma_start(y2c[:], y2_d[:, bass.ds(g * GT, GT)].rearrange("(m p) t -> p m t", p=P)).then_inc(yc_loaded, 16)

            def load_h1(g):
                sp.wait_ge(y_back, 2 * (g + 1))
                apart(sp, sp_waited)
                sp.dma_start(hin, rows(h_d, g)).then_inc(h_loaded, 16)

            def load_h(g, par):
                if first(g):
                    sp.wait_ge(y1_full, 4 * (G - 1))
                    sp.wait_ge(h2_stored, 16)
                elif isinstance(g, int) and g == 1:
                    sp.wait_ge(y1_full, 4 * G)
                need(sp, out_ready, g - 1)
                apart(sp, sp_waited)
                sp.dma_start(h3[par][:], rows(h2_d, g)).then_inc(h3_loaded[par], 16)

            def store_h2(g):
                sp.wait_ge(h2_ready, 2 * (g + 1))
                apart(sp, sp_waited)
                sp.dma_start(rows(h2_d, g), hin).then_inc(h2_stored, 16)

            def body2(g, half, par):
                load_q(g + 1, 1 - par)
                if not first(g):
                    load_k(g, 1)
                    store_y(g - 1)
                load_k(g + 1, 0)
                if not first(g):
                    load_h1(g - 1)
                    store_h2(g - 1)

            def last2(g, half, par):
                load_k(g, 1)
                store_y(g - 1)
                sp.wait_ge(y2_full, 4 * (G - 1))
                sp.dma_start(wi[:], w_in.rearrange("(m p) n -> p m n", p=P)).then_inc(w3_loaded, 16)
                sp.dma_start(wo[:], w_out.rearrange("(m p) n -> p m n", p=P)).then_inc(w3_loaded, 16)
                load_h(0, 0)
                load_h1(g - 1)
                store_h2(g - 1)
                store_y(g)

            groups(sp, lambda: None, body2, last2)

            def store(g, half, par):
                sp.wait_ge(out_ready, g + 1)
                apart(sp, sp_waited)
                sp.dma_start(rows(out, g), o3[par][:]).then_inc(out_stored[par], 16)

            def body3(g, half, par):
                if first(g):
                    load_h(1, 1)
                    load_h1(G - 1)
                    store_h2(G - 1)
                    sp.wait_ge(h2_stored, 16 * G)
                else:
                    load_h(g + 1, 1 - par)
                store(g, half, par)

            groups(sp, lambda: None, body3, store)
            for s in out_stored:
                sp.wait_ge(s, 16 * G // 2)

        @block.gpsimd
        def _(pool):
            pool.wait_ge(idx_loaded, 16)

            def gather(g, half, par):
                need(pool, h_made, g - 1)
                apart(pool, pool_waited)
                nc.gpsimd.tensor_copy(idx_g[par][:], idx_sb[:, bass.ds(g * TILES, TILES)]).then_inc(idx_ready, 1)
                pool.wait_ge(idx_ready, g + 1)
                apart(pool, pool_waited)
                for dst, table, done in ((staged_a, lora_a, gathered_a), (staged, tok_w, gathered)):
                    for i in range(TILES):
                        off = bass.IndirectOffsetOnAxis(ap=idx_g[par][:, i:i + 1].bitcast(U32), axis=0)
                        pool.indirect_dma_start(dst[par][:, i, :], None, table, off).then_inc(done[par], 16)

            gather(0, 0, 0)
            gather(1, 0, 1)
            with pool.Fori(0, 3) as i:
                gather(i * 2 + 2, i + 1, 0)
                gather(i * 2 + 3, i + 1, 1)

            pool.wait_ge(gathered[1], 16 * TILES * G // 2)
            for n in range(2):
                nc.gpsimd.memset(q_stack[n][KS:KS + 1, :, :], 1.0).then_inc(ones_ready, 1)
            nc.gpsimd.memset(r_stack[0:KS, T:SPAN], 0.0).then_inc(ones_ready, 1)
            nc.gpsimd.memset(r_stack[KS:KS + 1, 0:T], 0.0).then_inc(ones_ready, 1)
            nc.gpsimd.memset(r_stack[KS:KS + 1, T:SPAN], MASK).then_inc(ones_ready, 1)
            pool.wait_ge(ek_split, 1)
            for n, part in enumerate(K_PARTS):
                pool.dma_start(r_stack[n * HD:(n + 1) * HD, 0:T], ekp[:, part, :]).then_inc(ek_stacked, 16)

            def tail(g):
                pool.wait_ge(yc_loaded, 32 * (g + 1))
                nc.gpsimd.tensor_tensor(y1c[:], y1c[:], y2c[:], ALU.add).then_inc(y_summed, 1)
                pool.wait_ge(h_loaded, 16 * (g + 1))
                for a in range(2):
                    pool.wait_ge(proj_ready, 2 * g + a + 1)
                    rows_a = slice(2 * a, 2 * a + 2)
                    nc.gpsimd.tensor_tensor(hin[:, rows_a], hin[:, rows_a], yn[:, rows_a], ALU.add).then_inc(h2_ready, 1)

            tail(0)
            with pool.Fori(0, 3) as i:
                tail(i * 2 + 1)
                tail(i * 2 + 2)
            tail(G - 1)

        @block.scalar
        def _(act):
            def copy_at(g):
                act.wait_ge(a_transposed, g + 1)
                nc.scalar.activation(at[:], ps[0:RANK, 0, :], ACT.Copy).then_inc(at_copied, 1)

            def root1(g):
                act.wait_ge(var_ready, g + 1)
                nc.scalar.activation(ln[:, 1, :], ln[:, 0, :], ACT.Sqrt).then_inc(std_ready, 1)

            def round_xt(g, par):
                act.wait_ge(x_transposed, g + 1)
                nc.scalar.activation(xt_hi[par][:], ps[:, 3:5, :], ACT.Copy).then_inc(xt_rounded, 1)

            def copy_qk(g, u):
                act.wait_ge(qk_full, 4 * g + u + 1)
                need(act, qk_part3, 4 * g + u - 3)
                need(act, parts_stored[u], 16 * g)
                bias = small[:, u:u + 1] if u < 2 else small[:, 4 + u:5 + u]
                for dst in (x32[u][:], parts[u][:, 0, :]):
                    ins = nc.scalar.activation(dst, ps[:, 5 + u % 2, :], ACT.Identity, bias=bias,
                                               scale=1.0 if u < 2 else QK_SCALE)
                ins.then_inc(qk_copied, 1)

            def second_part(g, u):
                act.wait_ge(qk_rest, 4 * g + u + 1)
                nc.scalar.activation(parts[u][:, 1, :], rest[u % 2][:], ACT.Copy).then_inc(qk_part2, 1)

            def first1():
                copy_at(0)
                root1(0)
                copy_at(1)
                round_xt(0, 0)
                root1(1)

            def body1(g, half, par):
                if first(g):
                    copy_qk(g, 0)
                if not beyond(g + 1):
                    round_xt(g + 1, 1 - par)
                if not beyond(g + 2):
                    copy_at(g + 2)
                if not first(g):
                    copy_qk(g, 0)
                second_part(g, 0)
                copy_qk(g, 1)
                if not beyond(g + 2):
                    root1(g + 2)
                second_part(g, 1)
                copy_qk(g, 2)
                copy_qk(g, 3)
                second_part(g, 2)
                second_part(g, 3)

            act.wait_ge(consts, CONSTS)
            act.wait_ge(kb_ready, 1)
            act.wait_ge(w_loaded, 32)
            nc.scalar.activation(wa_hi[:], wa[:], ACT.Copy).then_inc(wa_rounded, 1)
            deep_groups(act, first1, body1)

            def root3(g):
                act.wait_ge(var3, g + 1)
                nc.scalar.activation(ln3[:, 1, :], ln3[:, 0, :], ACT.Sqrt).then_inc(std3, 1)

            def copy_att2(g, half, par, k):
                n = A_ORDER[k]
                if k % (A_USES // 4) == 0:
                    need(act, y2_full, 4 * (g - 2) + n + 1)
                act.wait_ge(att2_full, A_USES * g + k + 1)
                nc.scalar.activation(att[par][:, :, n * JC:(n + 1) * JC],
                                     ps[:, a_bank(g, k), :].rearrange("p (j x) -> p x j", x=BH), ACT.Copy).then_inc(att2_copied, 1)

            def exps(g, par, x):
                act.wait_ge(max_ready, BH * g + x + 1)
                need(act, pt_full, BH * g + x - 1)
                sc, pr = ps[:, 2 + x % 2, :], probs[x % 2]
                h, b = x // GB, x % GB
                nc.scalar.activation(pr[:, 0:P], sc[:, 0:P], ACT.Exp, bias=neg_max[:, x, 0:1],
                                     accum_out=sums[par][:, h, b, 0:1])
                nc.scalar.activation(pr[:, P:SPAN], sc[:, P:SPAN], ACT.Exp, bias=neg_max[:, x, 1:2],
                                     accum_out=sums[par][:, h, b, 1:2]).then_inc(exp_done, 1)

            def copy_pt(g, par, x):
                act.wait_ge(pt_full, BH * g + x + 1)
                nc.scalar.activation(att[par][:, x, :], ps[:, 4 + x % 2, 0:SPAN], ACT.Copy).then_inc(pt_copied[0], 1)

            def copy_y1(g, nb):
                act.wait_ge(y1_full, 4 * g + nb + 1)
                need(act, y1_stored, 64 * g)
                nc.scalar.activation(y1s[:, nb, :], ps[:, 6, :], ACT.Copy).then_inc(y1_copied, 1)

            def tail_yt(g, m):
                act.wait_ge(yt_full, 2 * g + m + 1)
                nc.scalar.activation(yt[:, m, :], ps[:, tail_bank(g), :], ACT.Copy).then_inc(yt_copied, 1)

            def y1_done(g, s):
                if s >= 13 and (s - 13) % BLOCK == 0:
                    copy_y1(g, (s - 13) // BLOCK)
                if s == 5 and not first(g):
                    copy_y1(g - 1, 3)

            def pairs(g, par, s):
                for gg, pp, x in lagged(g, par, s, 2):
                    exps(gg, pp, x)
                for gg, pp, x in lagged(g, par, s, 3):
                    if COPIES[x] == 0:
                        copy_pt(gg, pp, x)

            def attention(g, half, par, following):
                for s in range(BH):
                    if not first(g) and s - 1 in YT_AT:
                        tail_yt(g - 1, YT_AT.index(s - 1))
                    y1_done(g, s)
                    pairs(g, par, s)
                    if following and s in A_AT:
                        copy_att2(g + 1, half + par, 1 - par, A_AT[s])
                    if last(g):
                        round_w(s - ROUND_AT)

            def first2():
                for s, count in ((qk_full, 4 * G), (v_copied, 2 * G), (xt_ready, G), (h_stored[0], 8 * G), (h_stored[1], 8 * G)):
                    act.wait_ge(s, count)
                for k in range(0, A_USES, 2):
                    copy_att2(0, 0, 0, k)
                act.wait_ge(stage1_done, 1)

            def last2(g, half, par):
                attention(g, half, par, False)
                for s in range(5):
                    pairs(g + 1, 1 - par, s)
                    round_w(s + BH - ROUND_AT)
                copy_y1(g, 3)
                root3(0)
                act.wait_ge(w_split, PAR)
                act.dma_start(treef[:], tree_in).then_inc(tree_loaded, 16)

            def round_w(p):
                if not 0 <= p < PAR:
                    return
                if p == 0:
                    act.wait_ge(w3_loaded, 32)
                cols = slice(2 * P * p, 2 * P * (p + 1))
                nc.scalar.activation(wi_hi[:, :, cols], wi[:, :, cols], ACT.Copy)
                nc.scalar.activation(wo_hi[:, 2 * p:2 * p + 2, :], wo[:, 2 * p:2 * p + 2, :], ACT.Copy).then_inc(w_hi, 1)

            groups(act, first2, lambda g, half, par: attention(g, half, par, True), last2)

            def copy_x3(g, par):
                act.wait_ge(x3_transposed, g + 1)
                nc.scalar.activation(x_hi[par][:], ps[:, 0:2, :], ACT.Copy).then_inc(x_rounded, 1)

            def silus(g, p):
                for m in range(2):
                    if m == 0:
                        act.wait_ge(dec_ready, PAR * g + p + 1)
                    else:
                        act.wait_ge(logit_full, WT * g + 2 * p + 2)
                    need(act, masked_ready, WT * g + 2 * (p - 2) + m + 1)
                    nc.scalar.activation(acts[p % 2][m][:], ps[:, 2 + m, :], ACT.Silu,
                                         bias=small[:, 8 + 2 * p + m:9 + 2 * p + m]).then_inc(acts_ready, 1)

            def high(g, p):
                for m in range(2):
                    act.wait_ge(masked_ready, WT * g + 2 * p + m + 1)
                    need(act, ffn_full, PAR * g + p - 1)
                    nc.scalar.activation(m_hi[p % 2][m][:], masked[p % 2][m][:], ACT.Copy).then_inc(hi_ready, 1)

            def first3():
                copy_x3(0, 0)

            def trees(g, half, par, following):
                for p in range(PAR + 1):
                    if first(g) and p in TAIL_YT_AT:
                        tail_yt(G - 1, TAIL_YT_AT.index(p))
                    if p < PAR:
                        silus(g, p)
                    if p >= 1:
                        high(g, p - 1)
                    if p == 3 and following:
                        root3(g + 1)
                    if p == 7 and following:
                        copy_x3(g + 1, 1 - par)

            groups(act, first3, lambda g, half, par: trees(g, half, par, True),
                   lambda g, half, par: trees(g, half, par, False))

        @block.vector
        def _(dve):
            nc.vector.memset(ps[:, 6:8, :], 0.0).then_inc(psum_clear, 1)
            dve.wait_ge(consts, CONSTS)
            nc.vector.tensor_scalar(small[:, 6:8], small[:, 2:4], QK_SCALE, None, ALU.mult).then_inc(kb_ready, 1)

            dve.wait_ge(ek_loaded, 16)
            links = [0]

            def link(ins):
                links[0] += 1
                ins.then_inc(ek_chain, 1)
                dve.wait_ge(ek_chain, links[0])

            link(nc.vector.tensor_copy(ekp[:, 0, :], ek[:, 0, :]))
            link(nc.vector.tensor_tensor(ek[:, 1, :], ek[:, 0, :], ekp[:, 0, :], ALU.subtract))
            link(nc.vector.tensor_copy(ekp[:, 1, :], ek[:, 1, :]))
            nc.vector.tensor_tensor(ekp[:, 2, :], ek[:, 1, :], ekp[:, 1, :], ALU.subtract).then_inc(ek_split, 1)

            def front1(g, half, par, between=lambda: None):
                dve.wait_ge(gathered[par], 16 * TILES * (half + 1))
                dve.wait_ge(lora_ready, g + 1)
                need(dve, h_stored[par], 16 * half)
                for m in range(2):
                    ins = nc.vector.scalar_tensor_tensor(
                        h_new[par][:, 2 * m:2 * m + 2, :], ps[:, 1 + m, :].rearrange("p (i c) -> p i c", i=2), LORA_SCALE,
                        staged[par][:, 2 * m:2 * m + 2, :], ALU.mult, ALU.add)
                ins.then_inc(h_made, 1)
                dve.wait_ge(h_made, g + 1)
                need(dve, x_transposed, g)
                layer_norm(dve, g, h_new[par], stats, mv, ln, xn, var_ready, std_ready, xn_ready, dve_chain,
                           between)

            def rest_of(g, u):
                dve.wait_ge(qk_copied, 4 * g + u + 1)
                need(dve, qk_part3, 4 * g + u - 1)
                nc.vector.tensor_tensor(rest[u % 2][:], x32[u][:], parts[u][:, 0, :], ALU.subtract).then_inc(qk_rest, 1)

            def third_part(g, u):
                dve.wait_ge(qk_part2, 4 * g + u + 1)
                nc.vector.tensor_tensor(parts[u][:, 2, :], rest[u % 2][:], parts[u][:, 1, :], ALU.subtract).then_inc(qk_part3, 1)

            def low_xt(g, par):
                dve.wait_ge(xt_rounded, g + 1)
                nc.vector.tensor_tensor(xt_lo[par][:], ps[:, 3:5, :], xt_hi[par][:].bitcast(F32), ALU.subtract).then_inc(xt_ready, 1)

            def back1_v(g, half, par, m):
                dve.wait_ge(v_full, 2 * g + m + 1)
                nc.vector.tensor_tensor(v_out[par][:, 2 * m:2 * m + 2, :], ps[:, 7, :].rearrange("p (i c) -> p i c", i=2),
                                            vb[:, :].unsqueeze(1).to_broadcast([P, 2, C]), ALU.add).then_inc(v_copied, 1)

            def first1():
                dve.wait_ge(wa_rounded, 1)
                nc.vector.tensor_tensor(wa_lo[:], wa[:], wa_hi[:].bitcast(F32), ALU.subtract).then_inc(wa_split, 1)
                front1(0, 0, 0)
                low_xt(0, 0)
                front1(1, 0, 1)

            def body1(g, half, par):
                if first(g):
                    rest_of(g, 0)
                    back1_v(g, half, par, 0)
                if not beyond(g + 1):
                    low_xt(g + 1, 1 - par)
                if not first(g):
                    rest_of(g, 0)
                    back1_v(g, half, par, 0)

                def between():
                    third_part(g, 0)
                    rest_of(g, 1)

                if not beyond(g + 2):
                    front1(g + 2, half + 1, par, between)
                else:
                    between()
                third_part(g, 1)
                rest_of(g, 2)
                rest_of(g, 3)
                back1_v(g, half, par, 1)
                third_part(g, 2)
                third_part(g, 3)
                if not beyond(g + 1):
                    need(dve, v_stored[1 - par], 16 * (half + par))

            dve.wait_ge(w_loaded, 32)
            dve.wait_ge(psum_clear, 1)
            deep_groups(dve, first1, body1)

            def front3(g, half, par, between=lambda: None):
                dve.wait_ge(h3_loaded[par], 16 * (half + 1))
                need(dve, x3_transposed, g)
                layer_norm(dve, g, h3[par], stats3, mv3, ln3, xn3, var3, std3, xn3_ready, chain3, between)

            def add(g, half, par, x):
                dve.wait_ge(att1_full, BH * g + x + 1)
                if x == 0:
                    dve.wait_ge(att2_copied, att2_copies(g + 1))
                if first(g) and x == 0:
                    dve.wait_ge(att2_by_dve, A_USES // 2)
                row = att[par][:, x, :]
                nc.vector.tensor_tensor(row, ps[:, 0, 0:SPAN], row, ALU.add).then_inc(scores_ready, 1)

            def maxima(g, par, x):
                dve.wait_ge(st_full, BH * g + x + 1)
                nc.vector.tensor_reduce(neg_max[:, x, :], ps[:, 2 + x % 2, 0:SPAN].rearrange("p (n s) -> p n s", n=3),
                                        AX.X, ALU.max, negate=True).then_inc(maxes, 1)
                dve.wait_ge(maxes, BH * g + x + 1)
                nc.vector.tensor_tensor(neg_max[:, x, 1:2], neg_max[:, x, 1:2], neg_max[:, x, 2:3], ALU.min).then_inc(max_ready, 1)

            def copy_pt(g, par, x):
                dve.wait_ge(pt_full, BH * g + x + 1)
                nc.vector.tensor_copy(att[par][:, x, :], ps[:, 4 + x % 2, 0:SPAN]).then_inc(pt_copied[1], 1)

            def copy_y2(g, c):
                dve.wait_ge(y2_full, 4 * g + c + 1)
                need(dve, y2_stored, 128 * g)
                nc.vector.tensor_copy(y2s[:, :, c * JC:(c + 1) * JC],
                                      ps[:, y2_bank(g, c), :].rearrange("p (j x) -> p x j", x=BH)).then_inc(y2_copied, 1)

            def tail_norm(g, par, a):
                if a == 0:
                    flat = sums[par][:].rearrange("p h b j -> p (h b j)")
                    need(dve, h2_ready, 2 * g)
                    nc.vector.reciprocal(flat, flat).then_inc(inv_ready, 1)
                    dve.wait_ge(inv_ready, g + 1)
                dve.wait_ge(y_back, 2 * g + a + 1)
                for j in range(2):
                    ins = nc.vector.tensor_tensor(
                        yn[:, 2 * a + j, :].rearrange("p (h d) -> p h d", h=H),
                        ps[:, tail_bank(g), j * C:(j + 1) * C].rearrange("p (h d) -> p h d", h=H),
                        sums[par][:, :, a, j:j + 1].to_broadcast([P, H, HD]), ALU.mult)
                ins.then_inc(yn_ready, 1)

            def tail_proj(g, a):
                dve.wait_ge(proj_full, 2 * g + a + 1)
                nc.vector.tensor_tensor(yn[:, 2 * a:2 * a + 2, :], ps[:, tail_bank(g), :].rearrange("p (i c) -> p i c", i=2),
                                        bp[:, :].unsqueeze(1).to_broadcast([P, 2, C]), ALU.add).then_inc(proj_ready, 1)

            def pairs(g, par, s):
                for gg, pp, x in lagged(g, par, s, 1):
                    maxima(gg, pp, x)
                for gg, pp, x in lagged(g, par, s, 3):
                    if COPIES[x] == 1:
                        copy_pt(gg, pp, x)

            def attention(g, half, par):
                for s in range(BH):
                    if not first(g):
                        if s - 1 in BACK_AT:
                            tail_norm(g - 1, 1 - par, BACK_AT.index(s - 1))
                        if s - 1 in PROJ_AT[1::2]:
                            tail_proj(g - 1, PROJ_AT.index(s - 1) // 2)
                        if s in Y2_COPY_AT:
                            copy_y2(g - 1, Y2_COPY_AT.index(s))
                    add(g, half, par, s)
                    pairs(g, par, s)

            def last2(g, half, par):
                attention(g, half, par)
                for s in range(5):
                    pairs(g + 1, 1 - par, s)
                front3(0, 0, 0, lambda: split_w(g))

            def split_w(g):
                for p in range(PAR):
                    cols = slice(2 * P * p, 2 * P * (p + 1))
                    dve.wait_ge(w_hi, p + 1)
                    nc.vector.tensor_tensor(wi_lo[:, :, cols], wi[:, :, cols], wi_hi[:, :, cols].bitcast(F32), ALU.subtract)
                    nc.vector.tensor_tensor(wo_lo[:, 2 * p:2 * p + 2, :], wo[:, 2 * p:2 * p + 2, :],
                                            wo_hi[:, 2 * p:2 * p + 2, :].bitcast(F32), ALU.subtract).then_inc(w_split, 1)
                    if p % 2 == 1:
                        copy_y2(g, p // 2)
                dve.wait_ge(w_split, PAR)

            def first2():
                for s, count in ((qk_full, 4 * G), (v_copied, 2 * G), (xt_ready, G), (h_stored[0], 8 * G), (h_stored[1], 8 * G)):
                    dve.wait_ge(s, count)
                for k in range(1, A_USES, 2):
                    n = A_ORDER[k]
                    dve.wait_ge(att2_full, k + 1)
                    nc.vector.tensor_copy(att[0][:, :, n * JC:(n + 1) * JC],
                                          ps[:, a_bank(0, k), :].rearrange("p (j x) -> p x j", x=BH)).then_inc(att2_by_dve, 1)

            dve.wait_ge(w2_loaded, 48)
            groups(dve, first2, attention, last2)

            def decide(g, p):
                dve.wait_ge(logit_full, WT * g + 2 * p + 1)
                need(dve, reach_full, WT * g + 2 * (p - 1))
                b = small[:, 8 + 2 * p:9 + 2 * p]
                nc.vector.tensor_scalar(dec[p % 2][:], ps[:, 2, :], b, 0.0, ALU.add, ALU.is_gt).then_inc(dec_ready, 1)

            def mask(g, p):
                for m in range(2):
                    dve.wait_ge(reach_full, WT * g + 2 * p + m + 1)
                    dve.wait_ge(acts_ready, WT * g + 2 * p + m + 1)
                    need(dve, lo_ready, WT * g + 2 * (p - 2) + m + 1)
                    nc.vector.scalar_tensor_tensor(masked[p % 2][m][:], ps[:, 4 + m, :], small[:, 24 + m:25 + m],
                                                   acts[p % 2][m][:], ALU.is_ge, ALU.mult).then_inc(masked_ready, 1)

            def low(g, p):
                for m in range(2):
                    dve.wait_ge(hi_ready, WT * g + 2 * p + m + 1)
                    need(dve, ffn_full, PAR * g + p - 1)
                    nc.vector.tensor_tensor(m_lo[p % 2][m][:], masked[p % 2][m][:], m_hi[p % 2][m][:].bitcast(F32),
                                            ALU.subtract).then_inc(lo_ready, 1)

            def low_x3(g, par):
                dve.wait_ge(x_rounded, g + 1)
                nc.vector.tensor_tensor(x_lo[par][:], ps[:, 0:2, :], x_hi[par][:].bitcast(F32), ALU.subtract).then_inc(xt3_ready, 1)

            def finish(g, half, par):
                dve.wait_ge(ffn_full, PAR * (g + 1))
                for m in range(2):
                    ins = nc.vector.tensor_tensor(o3[par][:, 2 * m:2 * m + 2, :], ps[:, 6 + m, :].rearrange("p (i c) -> p i c", i=2),
                                                  h3[par][:, 2 * m:2 * m + 2, :], ALU.add)
                ins.then_inc(out_ready, 1)

            def trees(g, half, par, following):
                for p in range(PAR + 2):
                    if first(g) and p in TAIL_BACK_AT:
                        tail_norm(G - 1, 1, TAIL_BACK_AT.index(p))
                    if first(g) and p in TAIL_PROJ_AT:
                        tail_proj(G - 1, TAIL_PROJ_AT.index(p) // 2)
                    if p < PAR:
                        decide(g, p)
                    if 1 <= p <= PAR:
                        mask(g, p - 1)
                    if p >= 2:
                        low(g, p - 2)
                    if p == 3 and following:
                        front3(g + 1, half + par, 1 - par)
                    if p == 8 and following:
                        low_x3(g + 1, 1 - par)
                finish(g, half, par)
                if following:
                    need(dve, out_stored[1 - par], 16 * (half + par))

            def first3():
                low_x3(0, 0)
                dve.wait_ge(tree_loaded, 16)
                nc.vector.tensor_copy(tree[:], treef[:]).then_inc(tree_ready, 1)

            groups(dve, first3, lambda g, half, par: trees(g, half, par, True),
                   lambda g, half, par: trees(g, half, par, False))

        @block.tensor
        def _(pe):
            pe.wait_ge(consts, CONSTS)
            pe.wait_ge(w_loaded, 32)

            def front1_a(g, half, par):
                pe.wait_ge(gathered_a[par], 16 * TILES * (half + 1))
                need(pe, at_copied, g)
                need(pe, lora_ready, g)
                for i in range(TILES):
                    ins = nc.tensor.transpose(ps[0:RANK, 0, i * P:(i + 1) * P], staged_a[par][:, i, :], ident[:])
                ins.then_inc(a_transposed, 1)

            def front1_lora(g):
                pe.wait_ge(at_copied, g + 1)
                need(pe, h_made, g)
                for i in range(TILES):
                    ins = nc.tensor.matmul(ps[:, 1 + i // 2, (i % 2) * C:(i % 2 + 1) * C], at[:, i * P:(i + 1) * P],
                                           lb[:], start=True, stop=True)
                ins.then_inc(lora_ready, 1)

            def front1_x(g, half, par):
                pe.wait_ge(xn_ready, g + 1)
                need(pe, xt_ready, g)
                for m in range(CM):
                    for i in range(TILES):
                        ins = nc.tensor.transpose(ps[:, 3 + m, i * P:(i + 1) * P], xn[:, i, m * P:(m + 1) * P], ident[:])
                ins.then_inc(x_transposed, 1)

            def qk(g, half, par, u0, u1):
                for u in range(u0, u1):
                    need(pe, qk_copied, 4 * g + u - 1)
                    terms = [(a, b, m) for m in range(CM) for a, b in ((wa_hi, xt_hi), (wa_lo, xt_hi), (wa_hi, xt_lo))]
                    for n, (a, b, m) in enumerate(terms):
                        ins = nc.tensor.matmul(ps[:, 5 + u % 2, :], a[:, m, u * P:(u + 1) * P], b[par][:, m, :],
                                               start=(n == 0), stop=(n == len(terms) - 1))
                    ins.then_inc(qk_full, 1)

            def value(g, half, par, a):
                need(pe, v_copied, 2 * g + a)
                terms = [(x, w, m) for m in range(CM) for x, w in ((xt_hi, wa_hi), (xt_hi, wa_lo), (xt_lo, wa_hi))]
                for i in range(2):
                    t = 2 * a + i
                    for n, (x, w, m) in enumerate(terms):
                        ins = nc.tensor.matmul(ps[:, 7, i * C:(i + 1) * C], x[par][:, m, t * P:(t + 1) * P],
                                               w[:, m, 2 * C:3 * C], start=(n == 0), stop=(n == len(terms) - 1))
                ins.then_inc(v_full, 1)

            def first1():
                front1_a(0, 0, 0)
                front1_lora(0)
                front1_a(1, 0, 1)
                front1_x(0, 0, 0)
                front1_lora(1)
                pe.wait_ge(wa_split, 1)

            def body1(g, half, par):
                pe.wait_ge(xt_ready, g + 1)
                if first(g):
                    qk(g, half, par, 0, 1)
                    value(g, half, par, 0)
                if not beyond(g + 1):
                    front1_x(g + 1, half + par, 1 - par)
                if not beyond(g + 2):
                    front1_a(g + 2, half + 1, par)
                if not first(g):
                    qk(g, half, par, 0, 1)
                    value(g, half, par, 0)
                if not beyond(g + 2):
                    front1_lora(g + 2)
                qk(g, half, par, 1, 4)
                value(g, half, par, 1)

            pe.wait_ge(psum_clear, 1)
            deep_groups(pe, first1, body1)

            def relative_keys(g, half, par, k):
                if k == 0:
                    pe.wait_ge(q_loaded[par], 16 * len(Q_PARTS) * (half + 1))
                if first(g):
                    need(pe, att2_by_dve if k % 2 else att2_copied, (k - 4) // 2 + 1)
                else:
                    pe.wait_ge(att2_copied, att2_copies(g) + k)
                for j in range(JC):
                    col = A_ORDER[k] * JC + j
                    u = col if col < T else col - T
                    t = col if col < T else col - P
                    ins = nc.tensor.matmul(ps[:, a_bank(g, k), j * BH:(j + 1) * BH], r_stack[:, T - 1 - u:T - 1 - u + P],
                                           q_stack[par][:, :, t], start=True, stop=True)
                ins.then_inc(att2_full, 1)

            def keys(g, half, par, x):
                if x % (BH // 2) == 0:
                    pe.wait_ge(k_loaded[x // (BH // 2)], 16 * len(K_PARTS) * (g + 1))
                if first(g) and x == 0:
                    pe.wait_ge(att2_copied, A_USES // 2)
                    pe.wait_ge(att2_by_dve, A_USES // 2)
                need(pe, scores_ready, BH * g + x)
                nc.tensor.matmul(ps[:, 0, 0:T], k_stack[:, x, 0:P], q_stack[par][0:KS, x, :], start=True, stop=True)
                nc.tensor.matmul(ps[:, 0, T:SPAN], k_stack[:, x, P:T], q_stack[par][0:KS, x, P:T],
                                 start=True, stop=True).then_inc(att1_full, 1)

            def to_rows(g, par, x):
                pe.wait_ge(scores_ready, BH * g + x + 1)
                need(pe, exp_done, BH * g + x - 1)
                for n in range(3):
                    ins = nc.tensor.transpose(ps[:, 2 + x % 2, n * P:(n + 1) * P], att[par][:, x, n * P:(n + 1) * P], ident[:])
                ins.then_inc(st_full, 1)

            def to_columns(g, par, x):
                pe.wait_ge(exp_done, BH * g + x + 1)
                if x >= 2 or not first(g):
                    pe.wait_ge(*copied(g, x - 2))
                for n in range(3):
                    ins = nc.tensor.transpose(ps[:, 4 + x % 2, n * P:(n + 1) * P], probs[x % 2][:, n * P:(n + 1) * P], ident[:])
                ins.then_inc(pt_full, 1)

            def values(g, par, x, half=None):
                h, b = x // GB, x % GB
                q = h % 4
                if x == 0 and half is not None:
                    pe.wait_ge(v_loaded[par], 16 * (half + 1))
                if x % BLOCK == 0:
                    need(pe, y1_copied, 4 * g + x // BLOCK)
                pe.wait_ge(*copied(g, x))
                vh = v_in[par]
                nc.tensor.matmul(ps[32 * q:32 * q + HD, 6, b * T:(b + 1) * T], vh[:, 2 * b, h * HD:(h + 1) * HD],
                                 att[par][:, x, 0:T], start=(b == 0), stop=False, skip_group_check=True)
                ins = nc.tensor.matmul(ps[32 * q:32 * q + HD, 6, b * T + P:(b + 1) * T], vh[:, 2 * b + 1, h * HD:(h + 1) * HD],
                                       att[par][:, x, T:SPAN], start=False, stop=True, skip_group_check=True)
                if x % BLOCK == BLOCK - 1:
                    ins.then_inc(y1_full, 1)

            def relative_values(g, par, j0, j1):
                for n in range(j0, j1):
                    c, j = n // JC, n % JC
                    if n == 0:
                        for e in range(2):
                            pe.wait_ge(pt_copied[e], COPIES.count(e) * (g + 1))
                        need(pe, proj_ready, 2 * g)
                    elif j == 0:
                        pe.wait_ge(y2_copied, 4 * g + c - (1 if last(g) else 0))
                    for q in range(4):
                        t = q * QT + n
                        o = ps[32 * q:32 * q + HD, y2_bank(g, c), j * BH:(j + 1) * BH]
                        ins = nc.tensor.matmul(o, rv[:, T - 1 - t, :], att[par][:, :, t], start=(j == 0), stop=(t < P),
                                               skip_group_check=True)
                        if t >= P:
                            ins = nc.tensor.matmul(o, rv[:, T - 1 - (t - P), :], att[par][:, :, t + P], start=False, stop=True,
                                                   skip_group_check=True)
                    if j == JC - 1:
                        ins.then_inc(y2_full, 1)

            def tail_back(g, a):
                if a == 0:
                    pe.wait_ge(y_summed, g + 1)
                    pe.wait_ge(y2_copied, 4 * (g + 1))
                else:
                    pe.wait_ge(yn_ready, 2 * g + 1)
                for j in range(2):
                    for m in range(CM):
                        t = 2 * a + j
                        ins = nc.tensor.transpose(ps[:, tail_bank(g), j * C + m * P:j * C + (m + 1) * P], y1c[:, m, t * P:(t + 1) * P], ident[:])
                ins.then_inc(y_back, 1)

            def tail_yt(g, m):
                if m == 0:
                    pe.wait_ge(yn_ready, 2 * (g + 1))
                else:
                    pe.wait_ge(yt_copied, 2 * g + 1)
                for i in range(TILES):
                    ins = nc.tensor.transpose(ps[:, tail_bank(g), i * P:(i + 1) * P], yn[:, i, m * P:(m + 1) * P], ident[:])
                ins.then_inc(yt_full, 1)

            def tail_proj(g, t):
                if t == 0:
                    pe.wait_ge(yt_copied, 2 * (g + 1))
                if t == 2:
                    pe.wait_ge(proj_ready, 2 * g + 1)
                i = t % 2
                for m in range(CM):
                    ins = nc.tensor.matmul(ps[:, tail_bank(g), i * C:(i + 1) * C], yt[:, m, t * P:(t + 1) * P], wp[:, m, :],
                                           start=(m == 0), stop=(m == CM - 1))
                if i == 1:
                    ins.then_inc(proj_full, 1)

            def attention(g, half, par, following):
                for s in range(BH):
                    keys(g, half, par, s)
                    for gg, pp, x in lagged(g, par, s, 1):
                        to_rows(gg, pp, x)
                    if following and s in A_AT:
                        relative_keys(g + 1, half + par, 1 - par, A_AT[s])
                    for gg, pp, x in lagged(g, par, s, 3):
                        to_columns(gg, pp, x)
                    for gg, pp, x in lagged(g, par, s, 5):
                        values(gg, pp, x, half if s >= 5 else None)
                    if not first(g) and s in Y2_AT:
                        relative_values(g - 1, 1 - par, *Y2_AT[s])
                    if not first(g):
                        for step, at_steps in ((tail_back, BACK_AT), (tail_yt, YT_AT), (tail_proj, PROJ_AT)):
                            if s in at_steps:
                                step(g - 1, at_steps.index(s))

            def first2():
                for n in range(A_USES):
                    relative_keys(0, 0, 0, n)

            def last2(g, half, par):
                attention(g, half, par, False)
                for s in range(5):
                    for lag, step in ((1, to_rows), (3, to_columns), (5, values)):
                        for gg, pp, x in lagged(g + 1, 1 - par, s, lag):
                            if gg == g:
                                step(g, par, x)
                relative_values(g, par, 0, 4 * JC)

            pe.wait_ge(w2_loaded, 48)
            pe.wait_ge(ones_ready, 5)
            pe.wait_ge(ek_stacked, 16 * len(K_PARTS))
            groups(pe, first2, lambda g, half, par: attention(g, half, par, True), last2)

            def front3(g, half, par):
                pe.wait_ge(xn3_ready, g + 1)
                need(pe, xt3_ready, g)
                for m in range(CM):
                    for i in range(TILES):
                        ins = nc.tensor.transpose(ps[:, m, i * P:(i + 1) * P], xn3[:, i, m * P:(m + 1) * P], ident[:])
                ins.then_inc(x3_transposed, 1)

            def logits(g, par, p):
                for m in range(2):
                    need(pe, acts_ready, WT * g + 2 * (p - 1) + m + 1)
                    if m == 0:
                        need(pe, dec_ready, PAR * g + p)
                    if first(g) and m == 0:
                        pe.wait_ge(w_split, p + 1)
                    w = (2 * p + m) * P
                    terms = [(a, b, k) for k in range(CM) for a, b in ((wi_hi, x_hi), (wi_lo, x_hi), (wi_hi, x_lo))]
                    for n, (a, b, k) in enumerate(terms):
                        ins = nc.tensor.matmul(ps[:, 2 + m, :], a[:, k, w:w + P], b[par][:, k, :], start=(n == 0),
                                               stop=(n == len(terms) - 1))
                    ins.then_inc(logit_full, 1)

            def reach(g, p):
                if first(g) and p == 0:
                    pe.wait_ge(tree_ready, 1)
                pe.wait_ge(dec_ready, PAR * g + p + 1)
                for m in range(2):
                    need(pe, masked_ready, WT * g + 2 * (p - 1) + m + 1)
                    nc.tensor.matmul(ps[:, 4 + m, :], tree[:, m * P:(m + 1) * P], dec[p % 2][:], start=True, stop=True).then_inc(reach_full, 1)

            def combine(g, p):
                for m in range(2):
                    pe.wait_ge(lo_ready, WT * g + 2 * p + m + 1)
                    if p == 0 and m == 0:
                        need(pe, out_ready, g)
                    for i in range(TILES):
                        for n, (a, b) in enumerate(((m_hi, wo_hi), (m_hi, wo_lo), (m_lo, wo_hi))):
                            ins = nc.tensor.matmul(
                                ps[:, 6 + i // 2, (i % 2) * C:(i % 2 + 1) * C], a[p % 2][m][:, i * P:(i + 1) * P],
                                b[:, 2 * p + m, :], start=(p == 0 and m == 0 and i % 2 == 0 and n == 0),
                                stop=(p == PAR - 1 and m == 1 and n == 2), skip_group_check=True)
                ins.then_inc(ffn_full, 1)

            def trees(g, half, par, following):
                pe.wait_ge(xt3_ready, g + 1)
                for p in range(PAR + 3):
                    if first(g):
                        for step, at_trees in ((tail_back, TAIL_BACK_AT), (tail_yt, TAIL_YT_AT), (tail_proj, TAIL_PROJ_AT)):
                            for n, at_tree in enumerate(at_trees):
                                if at_tree == p:
                                    step(G - 1, n)
                    if p < PAR:
                        logits(g, par, p)
                    if 1 <= p <= PAR:
                        reach(g, p - 1)
                    if p >= 3:
                        combine(g, p - 3)
                    if p == 7 and following:
                        if first(g):
                            pe.wait_ge(proj_ready, 2 * G)
                        front3(g + 1, half, 1 - par)

            groups(pe, lambda: front3(0, 0, 0), lambda g, half, par: trees(g, half, par, True),
                   lambda g, half, par: trees(g, half, par, False))


def tree_constants():
    tree, turns = np.zeros((P, 2 * P), np.float32), np.zeros((2 * P,), np.float32)
    for n in range(2 ** (DEPTH + 1) - 1):
        col = n if n < P - 1 else n + 1
        at = n
        while at:
            up, right = (at - 1) // 2, at % 2 == 0
            tree[up, col] = 1.0 if right else -1.0
            turns[col] += right
            at = up
    return tree, np.ascontiguousarray((turns - 0.5).reshape(2, P).T)


def kernel(x, L0_tok_weight, L0_tok_lora_A, L0_tok_lora_B, L0_attn_Wattn, L0_attn_battn, L0_attn_Wproj,
           L0_attn_bproj, L0_attn_embk, L0_attn_embv, L0_ffn_W_in, L0_ffn_b_in, L0_ffn_W_out):
    import concourse.bacc as bacc
    from concourse.bass_utils import run_bass_kernel_spmd

    def by_tile(a):
        a = a.reshape(PAR, 2 * P - 1, -1)
        gap = np.zeros((PAR, 1, a.shape[2]), a.dtype)
        return np.concatenate([a[:, :P - 1], gap, a[:, P - 1:]], axis=1).reshape(WT * P, -1)

    x = np.asarray(x)
    tree, thresholds = tree_constants()
    embv = np.asarray(L0_attn_embv)
    arrays = {
        "idx": x.reshape(TOK // P, P).T,
        "tok_w": L0_tok_weight,
        "lora_a": L0_tok_lora_A,
        "lora_b": L0_tok_lora_B,
        "wattn": L0_attn_Wattn,
        "battn": np.asarray(L0_attn_battn).reshape(6, P).T,
        "vbias": np.asarray(L0_attn_battn)[2 * C:].reshape(1, C),
        "wproj": L0_attn_Wproj,
        "bproj": np.asarray(L0_attn_bproj).reshape(1, C),
        "embk_rev": np.asarray(L0_attn_embk)[::-1].T,
        "embv_pad": np.concatenate([embv[::-1], np.zeros((P - 1, HD), embv.dtype)]),
        "w_in": by_tile(np.asarray(L0_ffn_W_in)).T,
        "b_in": by_tile(np.asarray(L0_ffn_b_in)).reshape(WT, P).T,
        "w_out": by_tile(np.asarray(L0_ffn_W_out).T),
        "ident_in": np.eye(P, dtype=np.float32),
        "tree_in": tree,
        "thr_in": thresholds,
    }
    arrays = {k: np.ascontiguousarray(v) for k, v in arrays.items()}
    nc = bacc.Bacc("TRN2", target_bir_lowering=False, num_devices=1)
    args = [nc.dram_tensor(k, v.shape, mybir.dt.from_np(v.dtype), kind="ExternalInput").ap() for k, v in arrays.items()]
    out = nc.dram_tensor("out", (TOK, C), F32, kind="ExternalOutput").ap()
    tower_kernel(nc, *args, out)
    r = run_bass_kernel_spmd(nc, [arrays], core_ids=[0])
    return r.results[0]["out"].reshape(BATCH, T, C)
```
